# Optimizing a Trainium2 kernel written in Bass

```python
import numpy as np
import jax
import jax.numpy as jnp

def _softmax(x, axis=-1):
    return jax.nn.softmax(x, axis=axis)

def _gelu(x):
    return jax.nn.gelu(x, approximate=True)

def _silu(x):
    return jax.nn.silu(x)

def _sigmoid(x):
    return jax.nn.sigmoid(x)

def _layernorm(x, axis=-1, eps=1e-05):
    m = jnp.mean(x, axis=axis, keepdims=True)
    v = jnp.var(x, axis=axis, keepdims=True)
    return (x - m) / jnp.sqrt(v + eps)

def _scatter_add(tgt, idx, src, axis=0):
    return tgt.at[idx].add(src)

def _segment_sum(src, seg, n):
    return jax.ops.segment_sum(src, seg, n)
kernel_name = 'mk_dlrm_tower_d1_rec_r8_83f2f5'

def setup_inputs(seed: int=0):
    np.random.seed(seed)
    _w = jnp.asarray

    def _rec_inputs():
        import jax
        import jax.numpy as jnp
        _tk = jax.random.key(seed)
        dense_ctx = jax.random.normal(jax.random.fold_in(_tk, 190), (1024, 16), jnp.float32)
        ids = jnp.stack([jax.random.randint(jax.random.fold_in(_tk, 200 + f), (1024,), 0, v, jnp.int32) for f, v in enumerate([1000, 12500, 1250, 125000, 12500, 1250, 1250, 125000, 1000, 1000, 12500, 1000, 1250, 1000, 125000, 1250, 125000, 125000, 1250, 125000, 1250, 1250, 1250, 12500, 125000, 125000, 1250, 1250, 12500, 12500, 1000, 125000, 12500, 1000, 1250, 12500, 1250, 1250, 125000])], axis=1)
        tbl_0 = 0.05 * jax.random.normal(jax.random.fold_in(_tk, 500 + 0), (1000, 16), jnp.float32)
        tbl_1 = 0.05 * jax.random.normal(jax.random.fold_in(_tk, 500 + 1), (12500, 16), jnp.float32)
        tbl_2 = 0.05 * jax.random.normal(jax.random.fold_in(_tk, 500 + 2), (1250, 16), jnp.float32)
        tbl_3 = 0.05 * jax.random.normal(jax.random.fold_in(_tk, 500 + 3), (125000, 16), jnp.float32)
        tbl_4 = 0.05 * jax.random.normal(jax.random.fold_in(_tk, 500 + 4), (12500, 16), jnp.float32)
        tbl_5 = 0.05 * jax.random.normal(jax.random.fold_in(_tk, 500 + 5), (1250, 16), jnp.float32)
        tbl_6 = 0.05 * jax.random.normal(jax.random.fold_in(_tk, 500 + 6), (1250, 16), jnp.float32)
        tbl_7 = 0.05 * jax.random.normal(jax.random.fold_in(_tk, 500 + 7), (125000, 16), jnp.float32)
        tbl_8 = 0.05 * jax.random.normal(jax.random.fold_in(_tk, 500 + 8), (1000, 16), jnp.float32)
        tbl_9 = 0.05 * jax.random.normal(jax.random.fold_in(_tk, 500 + 9), (1000, 16), jnp.float32)
        tbl_10 = 0.05 * jax.random.normal(jax.random.fold_in(_tk, 500 + 10), (12500, 16), jnp.float32)
        tbl_11 = 0.05 * jax.random.normal(jax.random.fold_in(_tk, 500 + 11), (1000, 16), jnp.float32)
        tbl_12 = 0.05 * jax.random.normal(jax.random.fold_in(_tk, 500 + 12), (1250, 16), jnp.float32)
        tbl_13 = 0.05 * jax.random.normal(jax.random.fold_in(_tk, 500 + 13), (1000, 16), jnp.float32)
        tbl_14 = 0.05 * jax.random.normal(jax.random.fold_in(_tk, 500 + 14), (125000, 16), jnp.float32)
        tbl_15 = 0.05 * jax.random.normal(jax.random.fold_in(_tk, 500 + 15), (1250, 16), jnp.float32)
        tbl_16 = 0.05 * jax.random.normal(jax.random.fold_in(_tk, 500 + 16), (125000, 16), jnp.float32)
        tbl_17 = 0.05 * jax.random.normal(jax.random.fold_in(_tk, 500 + 17), (125000, 16), jnp.float32)
        tbl_18 = 0.05 * jax.random.normal(jax.random.fold_in(_tk, 500 + 18), (1250, 16), jnp.float32)
        tbl_19 = 0.05 * jax.random.normal(jax.random.fold_in(_tk, 500 + 19), (125000, 16), jnp.float32)
        tbl_20 = 0.05 * jax.random.normal(jax.random.fold_in(_tk, 500 + 20), (1250, 16), jnp.float32)
        tbl_21 = 0.05 * jax.random.normal(jax.random.fold_in(_tk, 500 + 21), (1250, 16), jnp.float32)
        tbl_22 = 0.05 * jax.random.normal(jax.random.fold_in(_tk, 500 + 22), (1250, 16), jnp.float32)
        tbl_23 = 0.05 * jax.random.normal(jax.random.fold_in(_tk, 500 + 23), (12500, 16), jnp.float32)
        tbl_24 = 0.05 * jax.random.normal(jax.random.fold_in(_tk, 500 + 24), (125000, 16), jnp.float32)
        tbl_25 = 0.05 * jax.random.normal(jax.random.fold_in(_tk, 500 + 25), (125000, 16), jnp.float32)
        tbl_26 = 0.05 * jax.random.normal(jax.random.fold_in(_tk, 500 + 26), (1250, 16), jnp.float32)
        tbl_27 = 0.05 * jax.random.normal(jax.random.fold_in(_tk, 500 + 27), (1250, 16), jnp.float32)
        tbl_28 = 0.05 * jax.random.normal(jax.random.fold_in(_tk, 500 + 28), (12500, 16), jnp.float32)
        tbl_29 = 0.05 * jax.random.normal(jax.random.fold_in(_tk, 500 + 29), (12500, 16), jnp.float32)
        tbl_30 = 0.05 * jax.random.normal(jax.random.fold_in(_tk, 500 + 30), (1000, 16), jnp.float32)
        tbl_31 = 0.05 * jax.random.normal(jax.random.fold_in(_tk, 500 + 31), (125000, 16), jnp.float32)
        tbl_32 = 0.05 * jax.random.normal(jax.random.fold_in(_tk, 500 + 32), (12500, 16), jnp.float32)
        tbl_33 = 0.05 * jax.random.normal(jax.random.fold_in(_tk, 500 + 33), (1000, 16), jnp.float32)
        tbl_34 = 0.05 * jax.random.normal(jax.random.fold_in(_tk, 500 + 34), (1250, 16), jnp.float32)
        tbl_35 = 0.05 * jax.random.normal(jax.random.fold_in(_tk, 500 + 35), (12500, 16), jnp.float32)
        tbl_36 = 0.05 * jax.random.normal(jax.random.fold_in(_tk, 500 + 36), (1250, 16), jnp.float32)
        tbl_37 = 0.05 * jax.random.normal(jax.random.fold_in(_tk, 500 + 37), (1250, 16), jnp.float32)
        tbl_38 = 0.05 * jax.random.normal(jax.random.fold_in(_tk, 500 + 38), (125000, 16), jnp.float32)
        _rk = jax.random.fold_in(_tk, 7)
        W_top1 = 0.0606339 * jax.random.normal(jax.random.fold_in(_tk, 801), (272, 512), jnp.float32)
        W_top2 = 0.0441942 * jax.random.normal(jax.random.fold_in(_tk, 802), (512, 256), jnp.float32)
        W_top3 = 0.0625 * jax.random.normal(jax.random.fold_in(_tk, 803), (256, 1), jnp.float32)
        b_top1 = jnp.zeros((512,), jnp.float32)
        b_top2 = jnp.zeros((256,), jnp.float32)
        return (dense_ctx, ids, tbl_0, tbl_1, tbl_2, tbl_3, tbl_4, tbl_5, tbl_6, tbl_7, tbl_8, tbl_9, tbl_10, tbl_11, tbl_12, tbl_13, tbl_14, tbl_15, tbl_16, tbl_17, tbl_18, tbl_19, tbl_20, tbl_21, tbl_22, tbl_23, tbl_24, tbl_25, tbl_26, tbl_27, tbl_28, tbl_29, tbl_30, tbl_31, tbl_32, tbl_33, tbl_34, tbl_35, tbl_36, tbl_37, tbl_38, W_top1, b_top1, W_top2, b_top2, W_top3)
    dense_ctx, ids, tbl_0, tbl_1, tbl_2, tbl_3, tbl_4, tbl_5, tbl_6, tbl_7, tbl_8, tbl_9, tbl_10, tbl_11, tbl_12, tbl_13, tbl_14, tbl_15, tbl_16, tbl_17, tbl_18, tbl_19, tbl_20, tbl_21, tbl_22, tbl_23, tbl_24, tbl_25, tbl_26, tbl_27, tbl_28, tbl_29, tbl_30, tbl_31, tbl_32, tbl_33, tbl_34, tbl_35, tbl_36, tbl_37, tbl_38, W_top1, b_top1, W_top2, b_top2, W_top3 = _rec_inputs()

    def _L0_rec_setup():
        import jax, jax.numpy as jnp
        import numpy as np
        B, F, D = (1024, 39, 16)
        HIDDEN = [128, 128, 128]

        def _cin(x, Ws, bs):
            F0 = x.shape[1]
            h = x
            outs = []
            n = len(Ws)
            for i, (W, b) in enumerate(zip(Ws, bs)):
                L = W.shape[-1]
                Fk = h.shape[1]
                Wr = W.reshape(F0, Fk, L)
                z = jnp.einsum('bfd,bgd->bfgd', x, h)
                cur = jax.nn.relu(jnp.einsum('bfgd,fgl->bld', z, Wr) + b[None, :, None])
                if i != n - 1:
                    h = cur[:, :L // 2]
                    direct = cur[:, L // 2:]
                else:
                    direct = cur
                outs.append(direct)
            return jnp.concatenate(outs, axis=1).sum(-1)
        key = jax.random.key(seed)
        ks = jax.random.split(key, 8)
        x = jax.random.normal(ks[0], (B, F, D), dtype=jnp.float32)
        field_nums = [F]
        Ws, bs = ([], [])
        for i, L in enumerate(HIDDEN):
            fan_in = field_nums[0] * field_nums[-1]
            lim = np.sqrt(6.0 / fan_in)
            Ws.append(jax.random.uniform(ks[1 + i], (fan_in, L), jnp.float32, -lim, lim))
            bs.append(jnp.zeros((L,), jnp.float32))
            field_nums.append(L // 2)
        return {'x': x, 'W0': Ws[0], 'W1': Ws[1], 'W2': Ws[2], 'b0': bs[0], 'b1': bs[1], 'b2': bs[2]}
    _L0_rec_all = _L0_rec_setup()
    _L0_rec_in = {k: v for k, v in _L0_rec_all.items() if k in ('W0', 'W1', 'W2', 'b0', 'b1', 'b2')}
    del _L0_rec_all
    return {'dense_ctx': dense_ctx, 'ids': ids, 'tbl_0': tbl_0, 'tbl_1': tbl_1, 'tbl_2': tbl_2, 'tbl_3': tbl_3, 'tbl_4': tbl_4, 'tbl_5': tbl_5, 'tbl_6': tbl_6, 'tbl_7': tbl_7, 'tbl_8': tbl_8, 'tbl_9': tbl_9, 'tbl_10': tbl_10, 'tbl_11': tbl_11, 'tbl_12': tbl_12, 'tbl_13': tbl_13, 'tbl_14': tbl_14, 'tbl_15': tbl_15, 'tbl_16': tbl_16, 'tbl_17': tbl_17, 'tbl_18': tbl_18, 'tbl_19': tbl_19, 'tbl_20': tbl_20, 'tbl_21': tbl_21, 'tbl_22': tbl_22, 'tbl_23': tbl_23, 'tbl_24': tbl_24, 'tbl_25': tbl_25, 'tbl_26': tbl_26, 'tbl_27': tbl_27, 'tbl_28': tbl_28, 'tbl_29': tbl_29, 'tbl_30': tbl_30, 'tbl_31': tbl_31, 'tbl_32': tbl_32, 'tbl_33': tbl_33, 'tbl_34': tbl_34, 'tbl_35': tbl_35, 'tbl_36': tbl_36, 'tbl_37': tbl_37, 'tbl_38': tbl_38, 'W_top1': W_top1, 'b_top1': b_top1, 'W_top2': W_top2, 'b_top2': b_top2, 'W_top3': W_top3, 'L0_rec_W0': _L0_rec_in['W0'], 'L0_rec_W1': _L0_rec_in['W1'], 'L0_rec_W2': _L0_rec_in['W2'], 'L0_rec_b0': _L0_rec_in['b0'], 'L0_rec_b1': _L0_rec_in['b1'], 'L0_rec_b2': _L0_rec_in['b2']}

def reference(dense_ctx, ids, tbl_0, tbl_1, tbl_2, tbl_3, tbl_4, tbl_5, tbl_6, tbl_7, tbl_8, tbl_9, tbl_10, tbl_11, tbl_12, tbl_13, tbl_14, tbl_15, tbl_16, tbl_17, tbl_18, tbl_19, tbl_20, tbl_21, tbl_22, tbl_23, tbl_24, tbl_25, tbl_26, tbl_27, tbl_28, tbl_29, tbl_30, tbl_31, tbl_32, tbl_33, tbl_34, tbl_35, tbl_36, tbl_37, tbl_38, W_top1, b_top1, W_top2, b_top2, W_top3, L0_rec_W0, L0_rec_W1, L0_rec_W2, L0_rec_b0, L0_rec_b1, L0_rec_b2):
    import jax
    import jax.numpy as jnp

    def _L0_rec_ref(x, W0, W1, W2, b0, b1, b2):
        import jax, jax.numpy as jnp
        import numpy as np
        B, F, D = (1024, 39, 16)
        HIDDEN = [128, 128, 128]

        def _cin(x, Ws, bs):
            F0 = x.shape[1]
            h = x
            outs = []
            n = len(Ws)
            for i, (W, b) in enumerate(zip(Ws, bs)):
                L = W.shape[-1]
                Fk = h.shape[1]
                Wr = W.reshape(F0, Fk, L)
                z = jnp.einsum('bfd,bgd->bfgd', x, h)
                cur = jax.nn.relu(jnp.einsum('bfgd,fgl->bld', z, Wr) + b[None, :, None])
                if i != n - 1:
                    h = cur[:, :L // 2]
                    direct = cur[:, L // 2:]
                else:
                    direct = cur
                outs.append(direct)
            return jnp.concatenate(outs, axis=1).sum(-1)
        return _cin(x, [W0, W1, W2], [b0, b1, b2])
    e = jnp.stack([tbl_0[ids[:, 0]], tbl_1[ids[:, 1]], tbl_2[ids[:, 2]], tbl_3[ids[:, 3]], tbl_4[ids[:, 4]], tbl_5[ids[:, 5]], tbl_6[ids[:, 6]], tbl_7[ids[:, 7]], tbl_8[ids[:, 8]], tbl_9[ids[:, 9]], tbl_10[ids[:, 10]], tbl_11[ids[:, 11]], tbl_12[ids[:, 12]], tbl_13[ids[:, 13]], tbl_14[ids[:, 14]], tbl_15[ids[:, 15]], tbl_16[ids[:, 16]], tbl_17[ids[:, 17]], tbl_18[ids[:, 18]], tbl_19[ids[:, 19]], tbl_20[ids[:, 20]], tbl_21[ids[:, 21]], tbl_22[ids[:, 22]], tbl_23[ids[:, 23]], tbl_24[ids[:, 24]], tbl_25[ids[:, 25]], tbl_26[ids[:, 26]], tbl_27[ids[:, 27]], tbl_28[ids[:, 28]], tbl_29[ids[:, 29]], tbl_30[ids[:, 30]], tbl_31[ids[:, 31]], tbl_32[ids[:, 32]], tbl_33[ids[:, 33]], tbl_34[ids[:, 34]], tbl_35[ids[:, 35]], tbl_36[ids[:, 36]], tbl_37[ids[:, 37]], tbl_38[ids[:, 38]]], axis=1)
    z = _L0_rec_ref(e, L0_rec_W0, L0_rec_W1, L0_rec_W2, L0_rec_b0, L0_rec_b1, L0_rec_b2)
    z = z.reshape(z.shape[0], -1)
    h = jnp.concatenate([z, dense_ctx], axis=1)
    h = jnp.maximum(h @ W_top1 + b_top1, 0.0)
    h = jnp.maximum(h @ W_top2 + b_top2, 0.0)
    y = h @ W_top3
    return y

_drawn_inputs = setup_inputs


def setup_inputs(seed=0):
    import zlib

    import numpy as np

    out = dict(_drawn_inputs(seed))
    spreads = {'b_top1': (0.0, 2.0),
     'b_top2': (0.0, 2.0),
     'L0_rec_b0': (0.0, 0.335),
     'L0_rec_b1': (0.0, 0.469),
     'L0_rec_b2': (0.0, 0.8)}
    factors = {'tbl_0': 8.0,
     'tbl_1': 8.0,
     'tbl_2': 8.0,
     'tbl_3': 8.0,
     'tbl_4': 8.0,
     'tbl_5': 8.0,
     'tbl_6': 8.0,
     'tbl_7': 8.0,
     'tbl_8': 8.0,
     'tbl_9': 8.0,
     'tbl_10': 8.0,
     'tbl_11': 8.0,
     'tbl_12': 8.0,
     'tbl_13': 8.0,
     'tbl_14': 8.0,
     'tbl_15': 8.0,
     'tbl_16': 8.0,
     'tbl_17': 8.0,
     'tbl_18': 8.0,
     'tbl_19': 8.0,
     'tbl_20': 8.0,
     'tbl_21': 8.0,
     'tbl_22': 8.0,
     'tbl_23': 8.0,
     'tbl_24': 8.0,
     'tbl_25': 8.0,
     'tbl_26': 8.0,
     'tbl_27': 8.0,
     'tbl_28': 8.0,
     'tbl_29': 8.0,
     'tbl_30': 8.0,
     'tbl_31': 8.0,
     'tbl_32': 8.0,
     'tbl_33': 8.0,
     'tbl_34': 8.0,
     'tbl_35': 8.0,
     'tbl_36': 8.0,
     'tbl_37': 8.0,
     'tbl_38': 8.0,
     'L0_rec_W0': 8.0,
     'L0_rec_W1': 5.693,
     'L0_rec_W2': 4.763,
     'dense_ctx': 8.0}
    for name, (base, spread) in spreads.items():
        noise = np.random.default_rng([zlib.crc32(name.encode()), seed]).standard_normal(out[name].shape)
        drawn = base * np.exp(spread * noise) if base else spread * noise
        out[name] = jnp.asarray(drawn.astype(out[name].dtype))
    for name, factor in factors.items():
        out[name] = (out[name] * factor).astype(out[name].dtype)
    return out
```

```python
from contextlib import ExitStack

import concourse.bass as bass
from concourse import mybir

F32 = mybir.dt.float32
F32R = mybir.dt.float32r
I32 = mybir.dt.int32
U32 = mybir.dt.uint32
ALU = mybir.AluOpType
ACT = mybir.ActivationFunctionType

P = 128
B, F, D = 1024, 39, 16
L, H = 128, 64
DENSE = 16
COLS = B * D
BLOCKS = B // P
CH = 512
DPC = CH // P
QS = D // DPC
CHUNKS = BLOCKS * QS
SHIFTS = (F + 1) // 2
SPT = P // F
P0 = SPT * F
T0 = -(-SHIFTS // SPT)
T1 = -(-F // 2)
XROWS = 2 * T0 * SPT + F
XROWS = F + SPT * T0
GT = 4
M1, M2 = 512, 256


class Job:

    def __init__(self, layer, t0, n, split):
        self.layer, self.t0, self.n, self.split = layer, t0, n, split
        self.parts = P0 if layer == 0 else P


SPLIT = {(0, 0), (1, 1), (1, 3), (2, 1), (2, 3), (2, 2)}


def layer_jobs(layer):
    tiles = T0 if layer == 0 else T1
    return [Job(layer, t, min(GT, tiles - t), (layer, t // GT) in SPLIT) for t in range(0, tiles, GT)]


NATIVE_RING, SPLIT_RING = 2, 2


def plan():
    first, chunk = layer_jobs(0), layer_jobs(1) + layer_jobs(0) + layer_jobs(2)
    start = {}
    for kind in (False, True):
        start[kind] = 0
        for j in first:
            if j.split == kind:
                j.n_before = start[kind]
                start[kind] += 1
    per = {}
    for kind in (False, True):
        per[kind] = 0
        for j in chunk:
            if j.split == kind:
                j.n_before = start[kind] + per[kind]
                per[kind] += 1
    assert per[False] % NATIVE_RING == 0 and per[True] % SPLIT_RING == 0
    return first, chunk, per


def cin_tower(nc, ids, tables, dense_t, w_top1, b_top1, w_top2, b_top2, w_top3,
              w0a, w0b, w1, w2, b0, b1, b2, out):
    first_jobs, chunk_jobs, PER = plan()
    n1, n0 = len(layer_jobs(1)), len(layer_jobs(0))
    jobs1, jobs0, jobs2 = chunk_jobs[:n1], chunk_jobs[n1:n1 + n0], chunk_jobs[n1 + n0:]
    x_dram = nc.dram_tensor("x_rows", (XROWS, COLS), F32, kind="Internal").ap()

    with ExitStack() as ctx:
        def sb(name, shape, dt=F32):
            return ctx.enter_context(nc.sbuf_tensor(name, shape, dt))

        def pb(name):
            return ctx.enter_context(nc.psum_tensor(name, [P, CH], F32))

        def sem(name):
            return ctx.enter_context(nc.semaphore(name))

        ids_all = sb("ids_all", [P, BLOCKS * F], I32)
        ids_now = sb("ids_now", [P, F], I32)
        emb = sb("emb", [P, F * D])
        x_t = sb("x_t", [F, D * P])
        ident = sb("ident", [P, P])
        x_self = sb("x_self", [P0, CH])
        x_shift = sb("x_shift", [P0, T0, CH])
        x_pair = sb("x_pair", [P, T1, CH])
        h1 = sb("h1", [P, CH])
        h2 = sb("h2", [P, CH])
        z_nat = [sb(f"z_nat{i}", [P, GT, CH]) for i in range(NATIVE_RING)]
        z_raw = [sb(f"z_raw{i}", [P, GT, CH]) for i in range(SPLIT_RING)]
        z_hi = [sb(f"z_hi{i}", [P, GT, CH], F32R) for i in range(SPLIT_RING)]
        z_lo = [sb(f"z_lo{i}", [P, GT, CH], F32R) for i in range(SPLIT_RING)]
        r01 = sb("r01", [P, CH])
        r2 = sb("r2", [P, CH])
        acc01 = sb("acc01", [P, CH])
        acc2 = sb("acc2", [P, CH])
        half = sb("half", [P, 2, CH // 2])
        sum01 = sb("sum01", [P, B])
        sum2 = sb("sum2", [P, B])
        dense = sb("dense", [DENSE, B])
        bias = [sb(f"bias{i}", [P, 1]) for i in range(3)]
        w0_sb = sb("w0_sb", [P0, T0, L])
        w_sb = [w0_sb, sb("w1_sb", [P, T1, L]), sb("w2_sb", [P, T1, L])]
        slot = {}
        for j in layer_jobs(0) + layer_jobs(1) + layer_jobs(2):
            if j.split:
                for t in range(j.t0, j.t0 + j.n):
                    slot[j.layer, t] = len(slot)
        w_hi = sb("w_hi", [P, len(slot), L], F32R)
        w_lo = sb("w_lo", [P, len(slot), L], F32R)

        wt1 = x_pair[:, 0:3, :]
        wt2 = x_pair[:, 3:5, :].rearrange("p a (k n) -> p (a k) n", n=M2)
        wt3 = x_pair[:, 5, 0:M2 // P]
        bt1 = x_pair[:, 6, 0:M1 // P]
        bt2 = x_pair[:, 6, 8:8 + M2 // P]
        hid1 = [z_nat[0], z_nat[1]]
        hid2 = [z_raw[0], z_raw[1]]
        y_sb = x_pair[0:1, 7:9, :].rearrange("p a n -> p (a n)")

        ps = [pb("ps_layer0"), pb("ps_layer1"), pb("ps_layer2")]
        ps_t = [pb("ps_t0"), pb("ps_t1")]
        ps_m = [pb("ps_m0"), pb("ps_m1")]

        ids_in = sem("ids_in")
        small_in = sem("small_in")
        w0_in = sem("w0_in")
        w_in = sem("w_in")
        w0_made = sem("w0_made")
        w_hi_made = sem("w_hi_made")
        w_split_made = sem("w_split_made")
        ident_zero = sem("ident_zero")
        ident_made = sem("ident_made")
        ids_copied = sem("ids_copied")
        emb_in = sem("emb_in")
        t_made = sem("t_made")
        t_copied = sem("t_copied")
        x_stored = sem("x_stored")
        x_self_in = sem("x_self_in")
        x_pair_in = [sem(f"x_pair_in{g}") for g in range(n1)]
        nat_made = sem("nat_made")
        nat_used = sem("nat_used")
        raw_made = sem("raw_made")
        hi_made = sem("hi_made")
        lo_made = sem("lo_made")
        pair_used = sem("pair_used")
        h_made = [sem("h1_made"), sem("h2_made")]
        ps0_free = sem("ps0_free")
        r01_made = sem("r01_made")
        r01_used = sem("r01_used")
        r2_made = sem("r2_made")
        r2_used = sem("r2_used")
        folded = sem("folded")
        top_in = sem("top_in")
        ps_m_made = sem("ps_m_made")
        ps_m_read = sem("ps_m_read")
        out_stored = sem("out_stored")
        ps_free = [ps0_free, r01_made, r2_made]
        passed = {nc.sync: sem("sp_passed"), nc.gpsimd: sem("pool_passed"), nc.tensor: sem("pe_passed")}

        def place(job, c):
            absent = job.layer == 2 and type(c) is int and c == CHUNKS - 1
            return job.n_before - absent * sum(j.split == job.split for j in jobs0)

        def count(job, c):
            return place(job, c) + 1 if c is None else c * PER[job.split] + place(job, c) + 1

        def wait_made(eng, job, c):
            wait_apart(eng, raw_made if job.split else nat_made, count(job, c))

        def wait_used(eng, job, c):
            ring = SPLIT_RING if job.split else NATIVE_RING
            eng.wait_ge(pair_used if job.split else nat_used, count(job, c) + ring)

        def wait_apart(eng, s, value):
            eng.wait_ge(s, value)
            eng.sem_inc(passed[eng], 1)

        def blocks(eng, body):
            with eng.Fori(0, BLOCKS - 1) as i:
                body(i, False)
            body(BLOCKS - 1, True)

        def x_cols(row0, dims, c):
            return bass.AP(x_dram.tensor, c * CH + row0 * COLS,
                           [[s * COLS, n] for s, n in dims] + [[1, CH]])

        block = ctx.enter_context(nc.Block())

        @block.sync
        def _(sp):
            sp.dma_start(ids_all[:].rearrange("p (a f) -> p a f", f=F),
                         ids.rearrange("(a p) f -> p a f", p=P)).then_inc(ids_in, 16)
            sp.dma_start(w0_sb[:], w0a).then_inc(w0_in, 16)
            sp.dma_start(z_raw[0][0:P0].rearrange("p a n -> p (a n)")[:, 0:T0 * L],
                         w0b.rearrange("p t l -> p (t l)")).then_inc(w0_in, 16)
            for w, dst in ((w1, w_sb[1]), (w2, w_sb[2])):
                full = F // 2
                sp.dma_start(dst[:, 0:full, :],
                             w[0:full * P, :].rearrange("(t p) l -> p t l", p=P)).then_inc(w_in, 16)
                sp.dma_start(dst[0:H, full, :], w[full * P:F * H, :]).then_inc(w_in, 16)
            for i, b in enumerate((b0, b1, b2)):
                sp.dma_start(bias[i][:], b.rearrange("(p o) -> p o", o=1)).then_inc(small_in, 16)
            sp.dma_start(dense[:], dense_t).then_inc(small_in, 16)

            def store_x(i):
                wait_apart(sp, t_copied, QS * (i + 1))
                cols = bass.AP(x_dram.tensor, i * (D * P), [[COLS, F], [1, D * P]])
                again = bass.AP(x_dram.tensor, i * (D * P) + F * COLS, [[COLS, XROWS - F], [1, D * P]])
                sp.dma_start(cols, x_t[:]).then_inc(x_stored, 16)
                sp.dma_start(again, x_t[0:XROWS - F, :]).then_inc(x_stored, 16)

            def load_shift(c):
                for j in range(SPT):
                    rows = slice(j * F, (j + 1) * F)
                    sp.dma_start(x_self[rows], x_cols(0, [[1, F]], c)).then_inc(x_self_in, 16)
                    sp.dma_start(x_shift[rows], x_cols(j, [[1, F], [SPT, T0]], c)).then_inc(x_self_in, 16)

            def load_pair(g, c):
                t = g * GT
                for odd in range(2):
                    sp.dma_start(x_pair[odd * H:(odd + 1) * H, t:t + GT, :],
                                 x_cols(2 * t + odd, [[0, H], [2, GT]], c)).then_inc(x_pair_in[g], 16)

            store_x(0)
            sp.wait_ge(x_stored, 32)
            load_shift(0)
            for g in range(n1):
                load_pair(g, 0)
            for j in first_jobs:
                wait_made(sp, j, None)

            def body(i, last):
                for q in range(QS):
                    c = i * QS + q
                    end = last and q == QS - 1
                    if q == QS - 1 and not last:
                        wait_apart(sp, x_stored, 32 * (i + 2))
                    if not end:
                        load_shift(c + 1)
                    if q == 2 and not last:
                        store_x(i + 1)
                    if not end:
                        for g, j in enumerate(jobs2):
                            wait_made(sp, j, c)
                            if g == 0:
                                for j0 in jobs0:
                                    wait_made(sp, j0, c)
                            load_pair(g, c + 1)

            blocks(sp, body)

            wait_made(sp, jobs2[-1], CHUNKS - 1)
            wait_made(sp, jobs2[-2], CHUNKS - 1)
            for k in range(2):
                sp.dma_start(wt1[:, k, :], w_top1[k * P:(k + 1) * P, :]).then_inc(top_in, 16)
            sp.dma_start(wt1[0:DENSE, 2, :], w_top1[2 * P:, :]).then_inc(top_in, 16)
            sp.dma_start(wt2, w_top2.rearrange("(k p) n -> p k n", p=P)).then_inc(top_in, 16)
            sp.dma_start(wt3, w_top3).then_inc(top_in, 16)
            sp.dma_start(bt1, b_top1).then_inc(top_in, 16)
            sp.dma_start(bt2, b_top2).then_inc(top_in, 16)
            sp.wait_ge(ps_m_read, 2 * (M1 + M2) // P + 2)
            sp.dma_start(out.rearrange("b o -> o b"), y_sb).then_inc(out_stored, 16)
            sp.wait_ge(out_stored, 16)

        @block.gpsimd
        def _(pool):
            nc.gpsimd.memset(ident[:], 0.0).then_inc(ident_zero, 1)
            pool.wait_ge(ident_zero, 1)
            nc.gpsimd.affine_select(out=ident[:], in_=ident[:], compare_op=ALU.not_equal, fill=1.0, base=0,
                                    pattern=[[-1, P]], channel_multiplier=1).then_inc(ident_made, 1)
            pool.sem_inc(r01_used, 1)
            pool.sem_inc(r2_used, 1)
            pool.wait_ge(ids_in, 16)

            def next_ids(i):
                if not (type(i) is int and i == 0):
                    wait_apart(pool, emb_in, 16 * F * i)
                nc.gpsimd.tensor_copy(ids_now[:], ids_all[:, bass.ds(i * F, F)]).then_inc(ids_copied, 1)
                wait_apart(pool, ids_copied, i + 1)

            def gather(f0, f1):
                for f in range(f0, f1):
                    nc.gpsimd.indirect_dma_start(
                        out=emb[:, f * D:(f + 1) * D], out_offset=None, in_=tables[f],
                        in_offset=bass.IndirectOffsetOnAxis(ap=ids_now[:, f:f + 1].bitcast(U32), axis=0),
                    ).then_inc(emb_in, 16)

            next_ids(0)
            gather(0, F)
            pool.wait_ge(t_made, QS)
            next_ids(1)
            gather(0, F // 2)

            def add(acc, r, q, made, used, c):
                wait_apart(pool, made, c + 2)
                if q == 0:
                    nc.gpsimd.tensor_copy(acc[:], r[:]).then_inc(used, 1)
                else:
                    nc.gpsimd.tensor_tensor(acc[:], acc[:], r[:], ALU.add).then_inc(used, 1)
                wait_apart(pool, used, c + 2)

            def body(i, last):
                for q in range(QS):
                    c = i * QS + q
                    add(acc01, r01, q, r01_made, r01_used, c)
                    if not last:
                        if q == 0:
                            gather(F // 2, F)
                        if q == 2:
                            wait_apart(pool, t_made, QS * (i + 2))
                    add(acc2, r2, q, r2_made, r2_used, c)
                for n, (acc, total) in enumerate(((acc01, sum01), (acc2, sum2))):
                    nc.gpsimd.tensor_tensor(half[:, n, :], acc[:, 0:CH // 2], acc[:, CH // 2:CH],
                                            ALU.add).then_inc(folded, 1)
                pool.wait_ge(folded, 4 * i + 2)
                for n, (acc, total) in enumerate(((acc01, sum01), (acc2, sum2))):
                    nc.gpsimd.tensor_tensor(total[:, bass.ds(i * P, P)], half[:, n, 0:P], half[:, n, P:2 * P],
                                            ALU.add).then_inc(folded, 1)

            with pool.Fori(0, BLOCKS - 2) as i:
                body(i, False)
                next_ids(i + 2)
                gather(0, F // 2)
            body(BLOCKS - 2, False)
            body(BLOCKS - 1, True)

        @block.scalar
        def _(act):
            for free in ps_free:
                act.sem_inc(free, 1)
            act.wait_ge(w0_made, 2)
            act.wait_ge(w_in, 64)
            for (layer, t), s in slot.items():
                rows = P0 if layer == 0 else P
                last_w = nc.scalar.activation(w_hi[0:rows, s, :], w_sb[layer][0:rows, t, :], ACT.Copy)
            last_w.then_inc(w_hi_made, 1)
            act.wait_ge(small_in, 64)

            def copy_x(i):
                if type(i) is not int:
                    act.wait_ge(x_stored, 32 * i)
                for k in range(QS):
                    act.wait_ge(t_made, QS * i + k + 1)
                    nc.scalar.activation(x_t[:, k * CH:(k + 1) * CH], ps_t[k % 2][0:F, :],
                                         ACT.Copy).then_inc(t_copied, 1)

            def split_hi(job, c):
                if job.split:
                    n = count(job, c)
                    act.wait_ge(raw_made, n)
                    act.wait_ge(pair_used, n)
                    k = place(job, c) % SPLIT_RING
                    nc.scalar.activation(z_hi[k][0:job.parts, 0:job.n, :], z_raw[k][0:job.parts, 0:job.n, :],
                                         ACT.Copy).then_inc(hi_made, 1)

            def relu_h(layer, h, last_job, c):
                wait_used(act, last_job, c)
                nc.scalar.activation(h[0:H, :], ps[layer][0:H, :], ACT.Relu, bias=bias[layer][0:H, :])
                nc.scalar.activation(h[H:P, :], ps[layer][0:H, :], ACT.Relu,
                                     bias=bias[layer][0:H, :]).then_inc(h_made[layer], 1)

            def relu_direct0(c):
                act.wait_ge(r01_used, c + 1)
                nc.scalar.activation(r01[0:H, :], ps[0][H:P, :], ACT.Relu,
                                     bias=bias[0][H:P, :]).then_inc(ps_free[0], 1)

            def relu2(c):
                wait_used(act, jobs2[-1], c)
                act.wait_ge(r2_used, c + 1)
                nc.scalar.activation(r2[:], ps[2][:], ACT.Relu, bias=bias[2][:]).then_inc(r2_made, 1)

            copy_x(0)
            for j in first_jobs:
                split_hi(j, None)
            relu_h(0, h1, first_jobs[-1], None)

            def body(i, last):
                for q in range(QS):
                    c = i * QS + q
                    end = last and q == QS - 1
                    relu_direct0(c)
                    for j in jobs1:
                        split_hi(j, c)
                    if not end:
                        for j in jobs0:
                            split_hi(j, c)
                    relu_h(1, h2, jobs1[-1], c)
                    nc.scalar.activation(r01[H:P, :], ps[1][H:P, :], ACT.Relu,
                                         bias=bias[1][H:P, :]).then_inc(r01_made, 1)
                    for g, j in enumerate(jobs2):
                        split_hi(j, c)
                        if g == 2 and not end:
                            relu_h(0, h1, jobs0[-1], c)
                    relu2(c)
                    if q == 1 and not last:
                        copy_x(i + 1)

            blocks(act, body)

            act.wait_ge(top_in, 7 * 16)
            n = 0
            for hid, b, ms in ((hid1, bt1, M1 // P), (hid2, bt2, M2 // P)):
                for half_b in range(2):
                    for m in range(ms):
                        act.wait_ge(ps_m_made, n + 1)
                        nc.scalar.activation(hid[half_b][:, m, :], ps_m[n % 2][:], ACT.Relu,
                                             bias=b[:, m:m + 1]).then_inc(ps_m_read, 1)
                        n += 1
            for half_b in range(2):
                act.wait_ge(ps_m_made, n + 1)
                nc.scalar.activation(y_sb[:, half_b * CH:(half_b + 1) * CH], ps_m[n % 2][0:1, :],
                                     ACT.Copy).then_inc(ps_m_read, 1)
                n += 1

        @block.vector
        def _(dve):
            dve.sem_inc(lo_made, SPLIT_RING)
            nc.vector.memset(w_sb[1][H:P, T1 - 1, :], 0.0)
            nc.vector.memset(w_sb[2][H:P, T1 - 1, :], 0.0).then_inc(w0_made, 1)
            dve.wait_ge(w0_in, 32)
            nc.vector.tensor_tensor(w0_sb[:].rearrange("p t l -> p (t l)"), w0_sb[:].rearrange("p t l -> p (t l)"),
                                    z_raw[0][0:P0].rearrange("p a n -> p (a n)")[:, 0:T0 * L],
                                    ALU.add).then_inc(w0_made, 1)
            dve.wait_ge(w_hi_made, 1)
            for (layer, t), s in slot.items():
                rows = P0 if layer == 0 else P
                last_w = nc.vector.tensor_tensor(w_lo[0:rows, s, :], w_sb[layer][0:rows, t, :],
                                                 w_hi[0:rows, s, :].bitcast(F32), ALU.subtract)
            last_w.then_inc(w_split_made, 1)

            def product(job, c, x, h):
                n = count(job, c)
                k = place(job, c)
                if job.split:
                    dst, made = z_raw[k % SPLIT_RING], raw_made
                    dve.wait_ge(lo_made, n)
                else:
                    dst, made = z_nat[k % NATIVE_RING], nat_made
                    dve.wait_ge(nat_used, n)
                rows = job.parts
                nc.vector.tensor_tensor(dst[0:rows, 0:job.n, :], x,
                                        h.rearrange("p (o n) -> p o n", o=1).broadcast_to([rows, job.n, CH]),
                                        ALU.mult).then_inc(made, 1)

            def split_lo(job, c):
                dve.wait_ge(hi_made, count(job, c))
                k = place(job, c) % SPLIT_RING
                rows = job.parts
                nc.vector.tensor_tensor(z_lo[k][0:rows, 0:job.n, :], z_raw[k][0:rows, 0:job.n, :],
                                        z_hi[k][0:rows, 0:job.n, :].bitcast(F32),
                                        ALU.subtract).then_inc(lo_made, 1)

            def layer(jobs, c, chunk_of_x, h, wait_x):
                pending = None
                for g, j in enumerate(jobs):
                    wait_x(g)
                    x = x_shift[:, j.t0:j.t0 + j.n, :] if j.layer == 0 else x_pair[:, j.t0:j.t0 + j.n, :]
                    product(j, c, x, h)
                    if pending is not None:
                        split_lo(pending, c)
                    pending = j if j.split else None
                if pending is not None:
                    split_lo(pending, c)

            def layer0(jobs, c, chunk):
                def wait_x(g):
                    if g == 0:
                        dve.wait_ge(x_self_in, 2 * SPT * 16 * (chunk + 1))
                layer(jobs, c, chunk, x_self[:], wait_x)

            layer0(first_jobs, None, 0)

            def body(i, last):
                for q in range(QS):
                    c = i * QS + q
                    dve.wait_ge(h_made[0], c + 1)
                    layer(jobs1, c, c, h1[:], lambda g: dve.wait_ge(x_pair_in[g], 32 * (c + 1)))
                    if not (last and q == QS - 1):
                        layer0(jobs0, c, c + 1)
                    dve.wait_ge(h_made[1], c + 1)
                    layer(jobs2, c, c, h2[:], lambda g: None)

            blocks(dve, body)

        @block.tensor
        def _(pe):
            pe.sem_inc(nat_used, NATIVE_RING)
            pe.sem_inc(pair_used, SPLIT_RING)
            pe.wait_ge(ident_made, 1)

            def transposes(i):
                wait_apart(pe, emb_in, 16 * F * (i + 1))
                rows = emb[:].rearrange("p (f d) -> p d f", d=D)
                for k in range(QS):
                    n = QS * i + k
                    if not (type(n) is int and n < 2):
                        wait_apart(pe, t_copied, n - 1)
                    for d in range(DPC):
                        last_t = nc.tensor.transpose(ps_t[k % 2][0:F, d * P:(d + 1) * P],
                                                     rows[:, k * DPC + d, :], ident[:])
                    last_t.then_inc(t_made, 1)

            def contract(jobs, c, bank, free):
                pe.wait_ge(ps_free[bank], free)
                for j in jobs:
                    rows = j.parts
                    n = count(j, c)
                    first, last = j is jobs[0], j is jobs[-1]
                    if j.split:
                        pe.wait_ge(lo_made, n + SPLIT_RING)
                        k = place(j, c) % SPLIT_RING
                        for t in range(j.n):
                            s = slot[j.layer, j.t0 + t]
                            for p, (w, z) in enumerate(((w_hi, z_hi), (w_lo, z_hi), (w_hi, z_lo))):
                                mm = nc.tensor.matmul(ps[bank][:], w[0:rows, s, :], z[k][0:rows, t, :],
                                                      start=first and t == 0 and p == 0,
                                                      stop=last and t == j.n - 1 and p == 2)
                        mm.then_inc(pair_used, 1)
                    else:
                        pe.wait_ge(nat_made, n)
                        k = place(j, c) % NATIVE_RING
                        for t in range(j.n):
                            mm = nc.tensor.matmul(ps[bank][:], w_sb[j.layer][0:rows, j.t0 + t, :],
                                                  z_nat[k][0:rows, t, :],
                                                  start=first and t == 0, stop=last and t == j.n - 1)
                        mm.then_inc(nat_used, 1)

            transposes(0)
            pe.wait_ge(w0_made, 2)
            pe.wait_ge(w_split_made, 1)
            contract(first_jobs, None, 0, 1)
            pe.wait_ge(w_in, 64)

            def body(i, last):
                for q in range(QS):
                    c = i * QS + q
                    contract(jobs1, c, 1, c + 1)
                    if not (last and q == QS - 1):
                        contract(jobs0, c, 0, c + 2)
                    contract(jobs2, c, 2, c + 1)
                    if q == 1 and not last:
                        transposes(i + 1)

            blocks(pe, body)

            pe.wait_ge(top_in, 7 * 16)
            pe.wait_ge(folded, 4 * BLOCKS)
            n = 0
            for half_b in range(2):
                cols = slice(half_b * CH, (half_b + 1) * CH)
                for m in range(M1 // P):
                    if n >= 2:
                        pe.wait_ge(ps_m_read, n - 1)
                    for k, (w, z) in enumerate(((wt1[:, 0], sum01), (wt1[:, 1], sum2), (wt1[0:DENSE, 2], dense))):
                        mm = nc.tensor.matmul(ps_m[n % 2][:], w[:, m * P:(m + 1) * P], z[:, cols],
                                              start=k == 0, stop=k == 2)
                    mm.then_inc(ps_m_made, 1)
                    n += 1
            for half_b in range(2):
                for m in range(M2 // P):
                    pe.wait_ge(ps_m_read, max(n - 1, (half_b + 1) * (M1 // P)))
                    for k in range(M1 // P):
                        mm = nc.tensor.matmul(ps_m[n % 2][:], wt2[:, k, m * P:(m + 1) * P], hid1[half_b][:, k, :],
                                              start=k == 0, stop=k == M1 // P - 1)
                    mm.then_inc(ps_m_made, 1)
                    n += 1
            for half_b in range(2):
                pe.wait_ge(ps_m_read, max(n - 1, 2 * M1 // P + (half_b + 1) * (M2 // P)))
                for k in range(M2 // P):
                    mm = nc.tensor.matmul(ps_m[n % 2][0:1, :], wt3[:, k:k + 1], hid2[half_b][:, k, :],
                                          start=k == 0, stop=k == M2 // P - 1)
                mm.then_inc(ps_m_made, 1)
                n += 1


def pair_rows():
    import numpy as np

    a = np.full((T0, SPT, F), -1)
    b = np.full((T0, SPT, F), -1)
    for t in range(T0):
        for j in range(SPT):
            s = t * SPT + j
            if s < SHIFTS:
                for f in range(F):
                    g = (f + s) % F
                    a[t, j, f] = f * F + g
                    if s:
                        b[t, j, f] = g * F + f
    return a, b


def kernel(**inputs):
    import numpy as np
    import concourse.bacc as bacc
    from concourse.bass_utils import run_bass_kernel_spmd

    nc = bacc.Bacc("TRN2", target_bir_lowering=False, num_devices=1)
    arrays = {}

    def give(name, a):
        a = np.ascontiguousarray(a)
        arrays[name] = a
        return nc.dram_tensor(name, a.shape, mybir.dt.from_np(a.dtype), kind="ExternalInput").ap()

    w0 = np.asarray(inputs["L0_rec_W0"])
    w0 = np.concatenate([w0, np.zeros((1, L), w0.dtype)])
    pairs = [w0[rows].transpose(1, 2, 0, 3).reshape(P0, T0, L) for rows in pair_rows()]
    args = [
        give("ids", np.asarray(inputs["ids"])),
        [give(f"tbl_{f}", np.asarray(inputs[f"tbl_{f}"])) for f in range(F)],
        give("dense_t", np.asarray(inputs["dense_ctx"]).T),
        give("w_top1", np.asarray(inputs["W_top1"])),
        give("b_top1", np.asarray(inputs["b_top1"]).reshape(M1 // P, P).T),
        give("w_top2", np.asarray(inputs["W_top2"])),
        give("b_top2", np.asarray(inputs["b_top2"]).reshape(M2 // P, P).T),
        give("w_top3", np.asarray(inputs["W_top3"]).reshape(M2 // P, P).T),
        give("w0a", pairs[0]),
        give("w0b", pairs[1]),
        give("w1", np.asarray(inputs["L0_rec_W1"])),
        give("w2", np.asarray(inputs["L0_rec_W2"])),
        give("b0", np.asarray(inputs["L0_rec_b0"])),
        give("b1", np.asarray(inputs["L0_rec_b1"])),
        give("b2", np.asarray(inputs["L0_rec_b2"])),
    ]
    out = nc.dram_tensor("y", (B, 1), F32, kind="ExternalOutput").ap()
    cin_tower(nc, *args, out)
    r = run_bass_kernel_spmd(nc, [arrays], core_ids=[0])
    return r.results[0]["y"]
```

```python
from contextlib import ExitStack

import concourse.bass as bass
from concourse import mybir

F32 = mybir.dt.float32
F32R = mybir.dt.float32r
I32 = mybir.dt.int32
U32 = mybir.dt.uint32
ALU = mybir.AluOpType
ACT = mybir.ActivationFunctionType

P = 128
B, F, D = 1024, 39, 16
L, H = 128, 64
DENSE = 16
COLS = B * D
BLOCKS = B // P
CH = 512
QS = 4
BC = P // QS
DPT = CH // P
CHUNKS = BLOCKS * QS
SHIFTS = (F + 1) // 2
SPT = P // F
P0 = SPT * F
T0 = -(-SHIFTS // SPT)
T1 = -(-F // 2)
XROWS = 2 * T0 * SPT + F
XROWS = F + SPT * T0
GT = 2
M1, M2 = 512, 256


NAT, SPLIT = range(2)
H_PSUM = False
LAG = 1
EARLY = 1
RING = (4, 4)


class Job:

    def __init__(self, layer, t0, n, kind):
        self.layer, self.t0, self.n, self.kind = layer, t0, n, kind
        self.split = kind != NAT
        self.parts = P0 if layer == 0 else P


KINDS = {0: "NSNN", 1: "NSNNSNNSNN", 2: "NSNNSNSNSN"}


def layer_jobs(layer):
    tiles = T0 if layer == 0 else T1
    return [Job(layer, t, min(GT, tiles - t), "NS".index(KINDS[layer][t // GT])) for t in range(0, tiles, GT)]


def plan():
    first, chunk = layer_jobs(0), layer_jobs(1) + layer_jobs(0) + layer_jobs(2)
    per = []
    for kind in (NAT, SPLIT):
        n = 0
        for j in first:
            if j.kind == kind:
                j.n_before = n
                n += 1
        start = n
        for j in chunk:
            if j.kind == kind:
                j.n_before = n
                n += 1
        per.append(n - start)
        assert per[kind] * QS % RING[kind] == 0
    return first, chunk, per


def cin_tower(nc, ids, tables, dense_t, w_top1, b_top1, w_top2, b_top2, w_top3,
              w0a, w0b, w1, w2, b0, b1, b2, out):
    first_jobs, chunk_jobs, PER = plan()
    n1, n0 = len(layer_jobs(1)), len(layer_jobs(0))
    jobs1, jobs0, jobs2 = chunk_jobs[:n1], chunk_jobs[n1:n1 + n0], chunk_jobs[n1 + n0:]
    x_dram = nc.dram_tensor("x_rows", (XROWS, COLS), F32, kind="Internal").ap()

    with ExitStack() as ctx:
        def sb(name, shape, dt=F32):
            return ctx.enter_context(nc.sbuf_tensor(name, shape, dt))

        def pb(name):
            return ctx.enter_context(nc.psum_tensor(name, [P, CH], F32))

        def sem(name):
            return ctx.enter_context(nc.semaphore(name))

        ids_all = sb("ids_all", [P, BLOCKS * F], I32)
        ids_now = sb("ids_now", [P, F], I32)
        emb = sb("emb", [P, F * D])
        x_t = sb("x_t", [F, D * P])
        ident = sb("ident", [P, P])
        x_self = sb("x_self", [P0, CH])
        x_shift = sb("x_shift", [P0, T0, CH])
        x_pair = sb("x_pair", [P, T1, CH])
        kinds = (NAT, SPLIT)
        z = [[sb(f"z{k}_{i}", [P, GT, CH]) for i in range(RING[k])] for k in kinds]
        z_hi = [sb(f"z_hi{i}", [P, GT, CH], F32R) for i in range(RING[SPLIT])]
        z_lo = [sb(f"z_lo{i}", [P, GT, CH], F32R) for i in range(RING[SPLIT])]
        r01 = sb("r01", [P, CH])
        r2 = sb("r2", [P, CH])
        fold = sb("fold", [P, CH])
        sum01 = sb("sum01", [P, B])
        sum2 = sb("sum2", [P, B])
        dense = sb("dense", [DENSE, B])
        bias = [sb(f"bias{i}", [P, 1]) for i in range(3)]
        all_jobs = layer_jobs(0) + layer_jobs(1) + layer_jobs(2)
        w_at, s_at, n_nat, n_split = {}, {}, 0, 0
        for j in all_jobs:
            if j.split:
                s_at[j.layer, j.t0] = n_split
                n_split += j.n
            else:
                w_at[j.layer, j.t0] = n_nat
                n_nat += j.n
        w_nat = sb("w_nat", [P, n_nat, L])
        w_hi = sb("w_hi", [P, n_split, L], F32R)
        w_lo = sb("w_lo", [P, n_split, L], F32R)
        stage = x_pair[:].rearrange("p t (a l) -> p (t a) l", l=L)
        w0_a, w0_b = stage[0:P0, 0:T0, :], stage[0:P0, T0:2 * T0, :]
        w_raw = stage[:, 2 * T0:2 * T0 + n_split, :]

        def w_dst(j):
            return w_raw[:, s_at[j.layer, j.t0]:][:, 0:j.n, :] if j.split else w_nat[:, w_at[j.layer, j.t0]:][:, 0:j.n, :]

        wt1 = x_pair[:, 0:3, :]
        wt2 = x_pair[:, 3:5, :].rearrange("p a (k n) -> p (a k) n", n=M2)
        wt3 = x_pair[:, 5, 0:M2 // P]
        bt1 = x_pair[:, 6, 0:M1 // P]
        bt2 = x_pair[:, 6, 8:8 + M2 // P]
        hid1 = [z[NAT][0:2], z[NAT][2:4]]
        hid2 = z[SPLIT]
        y_sb = x_pair[0:1, 7:9, :].rearrange("p a n -> p (a n)")

        h1, h2 = (pb("h1"), pb("h2")) if H_PSUM else (sb("h1", [P, CH]), sb("h2", [P, CH]))
        ps = [pb("ps_layer0"), pb("ps_layer1"), pb("ps_layer2")]
        ps_t = [pb("ps_t0"), pb("ps_t1")]
        ps_m = ps_t

        ids_in = sem("ids_in")
        small_in = sem("small_in")
        w0_in = sem("w0_in")
        w_in = sem("w_in")
        w0_made = sem("w0_made")
        pads_zero = sem("pads_zero")
        w_hi_made = sem("w_hi_made")
        w_split_made = sem("w_split_made")
        ident_zero = sem("ident_zero")
        ident_made = sem("ident_made")
        ids_copied = sem("ids_copied")
        emb_in = sem("emb_in")
        t_made = sem("t_made")
        t_copied = sem("t_copied")
        x_stored = sem("x_stored")
        x_self_in = sem("x_self_in")
        x_pair_in = [sem(f"x_pair_in{g}") for g in range(n1)]
        z_made = [sem(f"z_made{k}") for k in kinds]
        hi_made = sem("hi_made")
        lo_made = sem("lo_made")
        z_used = [sem(f"z_used{k}") for k in kinds]
        h_made = [sem("h1_made"), sem("h2_made")]
        ps0_free = sem("ps0_free")
        r01_made = sem("r01_made")
        r01_used = sem("r01_used")
        r2_made = sem("r2_made")
        r2_used = sem("r2_used")
        folded = sem("folded")
        top_in = sem("top_in")
        ps_m_made = sem("ps_m_made")
        ps_m_read = sem("ps_m_read")
        out_stored = sem("out_stored")
        ps_free = [ps0_free, r01_made, r2_made]
        passed = {nc.sync: sem("sp_passed"), nc.gpsimd: sem("pool_passed"), nc.tensor: sem("pe_passed")}

        W_DMAS = 2 * (n1 + 1)

        def place(job, c):
            absent = job.layer == 2 and type(c) is int and c == CHUNKS - 1
            return job.n_before - absent * sum(j.kind == job.kind for j in jobs0)

        def count(job, c):
            return place(job, c) + 1 if c is None else c * PER[job.kind] + place(job, c) + 1

        def ring(job, c, q):
            return (place(job, c) + (0 if c is None else q * PER[job.kind])) % RING[job.kind]

        def wait_made(eng, job, c):
            wait_apart(eng, z_made[job.kind], count(job, c))

        def wait_used(eng, job, c):
            eng.wait_ge(z_used[job.kind], count(job, c) + RING[job.kind])

        def wait_apart(eng, s, value):
            eng.wait_ge(s, value)
            eng.sem_inc(passed[eng], 1)

        def blocks(eng, body):
            with eng.Fori(0, BLOCKS - 1) as i:
                body(i, False)
            body(BLOCKS - 1, True)

        def x_cols(row0, dims, c):
            return bass.AP(x_dram.tensor, c * CH + row0 * COLS,
                           [[s * COLS, n] for s, n in dims] + [[1, CH]])

        block = ctx.enter_context(nc.Block())

        @block.sync
        def _(sp):
            sp.dma_start(ids_all[:].rearrange("p (a f) -> p a f", f=F),
                         ids.rearrange("(a p) f -> p a f", p=P)).then_inc(ids_in, 16)
            sp.dma_start(w0_a, w0a).then_inc(w0_in, 16)
            sp.dma_start(w0_b, w0b).then_inc(w0_in, 16)
            for w, jobs in ((w1, layer_jobs(1)), (w2, layer_jobs(2))):
                for j in jobs:
                    full = min(j.n, F // 2 - j.t0)
                    sp.dma_start(w_dst(j)[:, 0:full, :], w[j.t0 * P:(j.t0 + full) * P, :].rearrange(
                        "(t p) l -> p t l", p=P)).then_inc(w_in, 16)
                sp.dma_start(w_dst(j)[0:H, full, :], w[(T1 - 1) * P:F * H, :]).then_inc(w_in, 16)
            for i, b in enumerate((b0, b1, b2)):
                sp.dma_start(bias[i][:], b.rearrange("(p o) -> p o", o=1)).then_inc(small_in, 16)
            sp.dma_start(dense[:], dense_t).then_inc(small_in, 16)

            def store_x(i):
                wait_apart(sp, t_copied, QS * (i + 1))
                cols = bass.AP(x_dram.tensor, i * (D * P), [[COLS, F], [1, D * P]])
                again = bass.AP(x_dram.tensor, i * (D * P) + F * COLS, [[COLS, XROWS - F], [1, D * P]])
                sp.dma_start(cols, x_t[:]).then_inc(x_stored, 16)
                sp.dma_start(again, x_t[0:XROWS - F, :]).then_inc(x_stored, 16)

            def load_shift(c):
                for j in range(SPT):
                    rows = slice(j * F, (j + 1) * F)
                    sp.dma_start(x_self[rows], x_cols(0, [[1, F]], c)).then_inc(x_self_in, 16)
                    sp.dma_start(x_shift[rows], x_cols(j, [[1, F], [SPT, T0]], c)).then_inc(x_self_in, 16)

            def load_pair(g, c):
                t = g * GT
                for odd in range(2):
                    sp.dma_start(x_pair[odd * H:(odd + 1) * H, t:t + GT, :],
                                 x_cols(2 * t + odd, [[0, H], [2, GT]], c)).then_inc(x_pair_in[g], 16)

            store_x(0)
            sp.wait_ge(x_stored, 32)
            load_shift(0)
            sp.wait_ge(w_split_made, 1)
            for g in range(n1):
                load_pair(g, 0)
            for j in first_jobs:
                wait_made(sp, j, None)

            def body(i, last):
                for q in range(QS):
                    c = i * QS + q
                    end = last and q == QS - 1
                    if q == QS - 1 and not last:
                        wait_apart(sp, x_stored, 32 * (i + 2))
                    if not end:
                        load_shift(c + 1)
                    if q == 2 and not last:
                        store_x(i + 1)
                    if not end:
                        for g, j in enumerate(jobs2):
                            wait_made(sp, j, c)
                            if g == 0:
                                for j0 in jobs0:
                                    wait_made(sp, j0, c)
                            load_pair(g, c + 1)

            blocks(sp, body)

            wait_made(sp, jobs2[-1], CHUNKS - 1)
            wait_made(sp, jobs2[-2], CHUNKS - 1)
            for k in range(2):
                sp.dma_start(wt1[:, k, :], w_top1[k * P:(k + 1) * P, :]).then_inc(top_in, 16)
            sp.dma_start(wt1[0:DENSE, 2, :], w_top1[2 * P:, :]).then_inc(top_in, 16)
            sp.dma_start(wt2, w_top2.rearrange("(k p) n -> p k n", p=P)).then_inc(top_in, 16)
            sp.dma_start(wt3, w_top3).then_inc(top_in, 16)
            sp.dma_start(bt1, b_top1).then_inc(top_in, 16)
            sp.dma_start(bt2, b_top2).then_inc(top_in, 16)
            sp.wait_ge(ps_m_read, 2 * (M1 + M2) // P + 2)
            sp.dma_start(out.rearrange("b o -> o b"), y_sb).then_inc(out_stored, 16)
            sp.wait_ge(out_stored, 16)

        @block.gpsimd
        def _(pool):
            nc.gpsimd.memset(ident[:], 0.0).then_inc(ident_zero, 1)
            pool.wait_ge(ident_zero, 1)
            nc.gpsimd.affine_select(out=ident[:], in_=ident[:], compare_op=ALU.not_equal, fill=1.0, base=0,
                                    pattern=[[-1, P]], channel_multiplier=1).then_inc(ident_made, 1)
            pool.sem_inc(r01_used, 1)
            pool.sem_inc(r2_used, 1)
            pool.wait_ge(ids_in, 16)

            def next_ids(i):
                if not (type(i) is int and i == 0):
                    wait_apart(pool, emb_in, 16 * F * i)
                nc.gpsimd.tensor_copy(ids_now[:], ids_all[:, bass.ds(i * F, F)]).then_inc(ids_copied, 1)
                wait_apart(pool, ids_copied, i + 1)

            def gather(fields):
                for f in fields:
                    nc.gpsimd.indirect_dma_start(
                        out=emb[:, f * D:(f + 1) * D], out_offset=None, in_=tables[f],
                        in_offset=bass.IndirectOffsetOnAxis(ap=ids_now[:, f:f + 1].bitcast(U32), axis=0),
                    ).then_inc(emb_in, 16)

            next_ids(0)
            gather(range(F))
            pool.wait_ge(t_made, QS)
            next_ids(1)
            gather(range(F // 2))

            def sum_dims(which, total, r, made, used, c):
                wait_apart(pool, made, c + 2)
                n, level = CH // 2, 0
                nc.gpsimd.tensor_tensor(fold[:, 0:n], r[:, 0:n], r[:, n:2 * n], ALU.add).then_inc(used, 1)
                wait_apart(pool, used, c + 2)
                at = 0
                while n > 2 * BC:
                    n //= 2
                    nc.gpsimd.tensor_tensor(fold[:, at + 2 * n:at + 3 * n], fold[:, at:at + n],
                                            fold[:, at + n:at + 2 * n], ALU.add).then_inc(folded, 1)
                    at, level = at + 2 * n, level + 1
                    wait_apart(pool, folded, c * 6 + which * 3 + level)
                nc.gpsimd.tensor_tensor(total[:, bass.ds(c * BC, BC)], fold[:, at:at + BC],
                                        fold[:, at + BC:at + 2 * BC], ALU.add).then_inc(folded, 1)
                wait_apart(pool, folded, c * 6 + which * 3 + 3)

            share = [range(F * n // QS, F * (n + 1) // QS) for n in (2, 3, 0, 1)]

            def body(i, last, last_gather):
                for q in range(QS):
                    c = i * QS + q
                    gathers = [] if last_gather and (q >= 2 or last) else list(share[q])
                    if q == 2 and gathers:
                        wait_apart(pool, t_made, QS * (i + 2))
                        next_ids(i + 2)
                    sum_dims(0, sum01, r01, r01_made, r01_used, c)
                    gather(gathers)
                    sum_dims(1, sum2, r2, r2_made, r2_used, c)

            with pool.Fori(0, BLOCKS - 2) as i:
                body(i, False, False)
            body(BLOCKS - 2, False, True)
            body(BLOCKS - 1, True, True)

        @block.scalar
        def _(act):
            for free in ps_free:
                act.sem_inc(free, 1)
            act.wait_ge(w0_made, 2)
            act.wait_ge(w_in, W_DMAS * 16)
            nc.scalar.activation(w_hi[:], w_raw, ACT.Copy).then_inc(w_hi_made, 1)
            act.wait_ge(small_in, 64)

            def copy_x(i):
                if type(i) is not int:
                    act.wait_ge(x_stored, 32 * i)
                for k in range(QS):
                    act.wait_ge(t_made, QS * i + k + 1)
                    rows = x_t[:].rearrange("f (q d b) -> f d q b", q=QS, d=D)
                    nc.scalar.activation(rows[:, k * DPT:(k + 1) * DPT],
                                         ps_t[k % 2][0:F, :].rearrange("f (d q b) -> f d q b", q=QS, b=BC),
                                         ACT.Copy).then_inc(t_copied, 1)

            def split_hi(job, c, q):
                if job.split:
                    n, kind = count(job, c), job.kind
                    act.wait_ge(z_made[kind], n)
                    act.wait_ge(z_used[kind], n)
                    k = ring(job, c, q)
                    nc.scalar.activation(z_hi[k][0:job.parts, 0:job.n, :], z[kind][k][0:job.parts, 0:job.n, :],
                                         ACT.Copy).then_inc(hi_made, 1)

            def relu_h(layer, h, last_job, c):
                wait_used(act, last_job, c)
                nc.scalar.activation(h[0:H, :], ps[layer][0:H, :], ACT.Relu, bias=bias[layer][0:H, :])
                nc.scalar.activation(h[H:P, :], ps[layer][0:H, :], ACT.Relu,
                                     bias=bias[layer][0:H, :]).then_inc(h_made[layer], 1)

            def relu_direct0(c):
                act.wait_ge(r01_used, c + 1)
                nc.scalar.activation(r01[0:H, :], ps[0][H:P, :], ACT.Relu,
                                     bias=bias[0][H:P, :]).then_inc(ps_free[0], 1)

            def relu2(c):
                wait_used(act, jobs2[-1], c)
                act.wait_ge(r2_used, c + 1)
                nc.scalar.activation(r2[:], ps[2][:], ACT.Relu, bias=bias[2][:]).then_inc(r2_made, 1)

            early = [j for j in jobs1 if j.split][:EARLY]
            copy_x(0)
            for j in first_jobs:
                split_hi(j, None, 0)
            relu_h(0, h1, first_jobs[-1], None)
            for j in early:
                split_hi(j, 0, 0)

            def body(i, last):
                for q in range(QS):
                    c = i * QS + q
                    end = last and q == QS - 1
                    relu_direct0(c)
                    for j in jobs1:
                        if j not in early:
                            split_hi(j, c, q)
                    if not end:
                        for j in jobs0:
                            split_hi(j, c, q)
                    relu_h(1, h2, jobs1[-1], c)
                    nc.scalar.activation(r01[H:P, :], ps[1][H:P, :], ACT.Relu,
                                         bias=bias[1][H:P, :]).then_inc(r01_made, 1)
                    for g, j in enumerate(jobs2):
                        split_hi(j, c, q)
                        if g == len(jobs2) // 2 and not end:
                            relu_h(0, h1, jobs0[-1], c)
                    if not end:
                        for j in early:
                            split_hi(j, c + 1, q + 1)
                    relu2(c)
                    if q == 1 and not last:
                        copy_x(i + 1)

            blocks(act, body)

            act.wait_ge(top_in, 7 * 16)
            n = 0
            for half_b in range(2):
                for m in range(M1 // P):
                    act.wait_ge(ps_m_made, n + 1)
                    nc.scalar.activation(hid1[half_b][m // 2][:, m % 2, :], ps_m[n % 2][:], ACT.Relu,
                                         bias=bt1[:, m:m + 1]).then_inc(ps_m_read, 1)
                    n += 1
            for half_b in range(2):
                for m in range(M2 // P):
                    act.wait_ge(ps_m_made, n + 1)
                    nc.scalar.activation(hid2[half_b][:, m, :], ps_m[n % 2][:], ACT.Relu,
                                         bias=bt2[:, m:m + 1]).then_inc(ps_m_read, 1)
                    n += 1
            for half_b in range(2):
                act.wait_ge(ps_m_made, n + 1)
                nc.scalar.activation(y_sb[:, half_b * CH:(half_b + 1) * CH], ps_m[n % 2][0:1, :],
                                     ACT.Copy).then_inc(ps_m_read, 1)
                n += 1

        @block.vector
        def _(dve):
            dve.sem_inc(lo_made, RING[SPLIT])
            nc.vector.memset(w_dst(jobs1[-1])[H:P, jobs1[-1].n - 1, :], 0.0)
            pads = nc.vector.memset(w_dst(jobs2[-1])[H:P, jobs2[-1].n - 1, :], 0.0)
            for j in first_jobs:
                if j.split:
                    pads = nc.vector.memset(w_dst(j)[96:P], 0.0)
            pads.then_inc(pads_zero, 1)
            dve.wait_ge(pads_zero, 1)
            dve.wait_ge(w0_in, 32)
            for j in first_jobs:
                w0_sum = nc.vector.tensor_tensor(w_dst(j)[0:P0], w0_a[:, j.t0:j.t0 + j.n, :],
                                                 w0_b[:, j.t0:j.t0 + j.n, :], ALU.add)
            w0_sum.then_inc(w0_made, 2)
            dve.wait_ge(w_hi_made, 1)
            nc.vector.tensor_tensor(w_lo[:], w_raw, w_hi[:].bitcast(F32), ALU.subtract).then_inc(w_split_made, 1)

            def product(job, c, q, x, h):
                n, k = count(job, c), ring(job, c, q)
                if job.split:
                    dve.wait_ge(lo_made, n)
                else:
                    dve.wait_ge(z_used[NAT], n)
                rows = job.parts
                nc.vector.tensor_tensor(z[job.kind][k][0:rows, 0:job.n, :], x,
                                        h.rearrange("p (o n) -> p o n", o=1).broadcast_to([rows, job.n, CH]),
                                        ALU.mult).then_inc(z_made[job.kind], 1)

            def split_lo(job, c, q):
                dve.wait_ge(hi_made, count(job, c))
                k, rows = ring(job, c, q), job.parts
                nc.vector.tensor_tensor(z_lo[k][0:rows, 0:job.n, :], z[SPLIT][k][0:rows, 0:job.n, :],
                                        z_hi[k][0:rows, 0:job.n, :].bitcast(F32),
                                        ALU.subtract).then_inc(lo_made, 1)

            def layer(jobs, c, q, h, wait_x):
                pending = []
                for g, j in enumerate(jobs):
                    wait_x(g)
                    x = x_shift[:, j.t0:j.t0 + j.n, :] if j.layer == 0 else x_pair[:, j.t0:j.t0 + j.n, :]
                    product(j, c, q, x, h)
                    if j.kind == SPLIT:
                        pending.append((g, j))
                    if pending and pending[0][0] <= g - LAG:
                        split_lo(pending.pop(0)[1], c, q)
                for _, j in pending:
                    split_lo(j, c, q)

            def layer0(jobs, c, q, chunk):
                def wait_x(g):
                    if g == 0:
                        dve.wait_ge(x_self_in, 2 * SPT * 16 * (chunk + 1))
                layer(jobs, c, q, x_self[:], wait_x)

            layer0(first_jobs, None, 0, 0)

            def body(i, last):
                for q in range(QS):
                    c = i * QS + q
                    dve.wait_ge(h_made[0], c + 1)
                    layer(jobs1, c, q, h1[:], lambda g: dve.wait_ge(x_pair_in[g], 32 * (c + 1)))
                    if not (last and q == QS - 1):
                        layer0(jobs0, c, q, c + 1)
                    dve.wait_ge(h_made[1], c + 1)
                    layer(jobs2, c, q, h2[:], lambda g: None)

            blocks(dve, body)

        @block.tensor
        def _(pe):
            for k in kinds:
                pe.sem_inc(z_used[k], RING[k])
            pe.wait_ge(ident_made, 1)

            def transposes(i):
                wait_apart(pe, emb_in, 16 * F * (i + 1))
                rows = emb[:].rearrange("p (f d) -> p d f", d=D)
                for k in range(QS):
                    n = QS * i + k
                    if not (type(n) is int and n < 2):
                        wait_apart(pe, t_copied, n - 1)
                    for d in range(DPT):
                        last_t = nc.tensor.transpose(ps_t[k % 2][0:F, d * P:(d + 1) * P],
                                                     rows[:, k * DPT + d, :], ident[:])
                    last_t.then_inc(t_made, 1)

            def contract(jobs, c, q, bank, free):
                pe.wait_ge(ps_free[bank], free)
                for j in jobs:
                    n, k, rows = count(j, c), ring(j, c, q), j.parts
                    if j.split:
                        pe.wait_ge(lo_made, n + RING[j.kind])
                        s = s_at[j.layer, j.t0]
                        passes = ((w_hi, s, z_hi[k]), (w_lo, s, z_hi[k]), (w_hi, s, z_lo[k]))
                    else:
                        pe.wait_ge(z_made[NAT], n)
                        passes = ((w_nat, w_at[j.layer, j.t0], z[NAT][k]),)
                    for t in range(j.n):
                        for p, (w, at, v) in enumerate(passes):
                            mm = nc.tensor.matmul(
                                ps[bank][:], w[0:rows, at + t, :], v[0:rows, t, :],
                                start=j is jobs[0] and t == 0 and p == 0,
                                stop=j is jobs[-1] and t == j.n - 1 and p == len(passes) - 1)
                    mm.then_inc(z_used[j.kind], 1)

            transposes(0)
            pe.wait_ge(w0_made, 2)
            pe.wait_ge(w_split_made, 1)
            contract(first_jobs, None, 0, 0, 1)
            pe.wait_ge(w_in, W_DMAS * 16)

            def body(i, last):
                for q in range(QS):
                    c = i * QS + q
                    contract(jobs1, c, q, 1, c + 1)
                    if not (last and q == QS - 1):
                        contract(jobs0, c, q, 0, c + 2)
                    contract(jobs2, c, q, 2, c + 1)
                    if q == 1 and not last:
                        transposes(i + 1)

            blocks(pe, body)

            pe.wait_ge(top_in, 7 * 16)
            pe.wait_ge(folded, 6 * CHUNKS)
            n = 0
            for half_b in range(2):
                cols = slice(half_b * CH, (half_b + 1) * CH)
                for m in range(M1 // P):
                    if n >= 2:
                        pe.wait_ge(ps_m_read, n - 1)
                    for k, (w, maps) in enumerate(((wt1[:, 0], sum01), (wt1[:, 1], sum2), (wt1[0:DENSE, 2], dense))):
                        mm = nc.tensor.matmul(ps_m[n % 2][:], w[:, m * P:(m + 1) * P], maps[:, cols],
                                              start=k == 0, stop=k == 2)
                    mm.then_inc(ps_m_made, 1)
                    n += 1
            for half_b in range(2):
                for m in range(M2 // P):
                    pe.wait_ge(ps_m_read, max(n - 1, (half_b + 1) * (M1 // P)))
                    for k in range(M1 // P):
                        mm = nc.tensor.matmul(ps_m[n % 2][:], wt2[:, k, m * P:(m + 1) * P], hid1[half_b][k // 2][:, k % 2, :],
                                              start=k == 0, stop=k == M1 // P - 1)
                    mm.then_inc(ps_m_made, 1)
                    n += 1
            for half_b in range(2):
                pe.wait_ge(ps_m_read, max(n - 1, 2 * M1 // P + (half_b + 1) * (M2 // P)))
                for k in range(M2 // P):
                    mm = nc.tensor.matmul(ps_m[n % 2][0:1, :], wt3[:, k:k + 1], hid2[half_b][:, k, :],
                                          start=k == 0, stop=k == M2 // P - 1)
                mm.then_inc(ps_m_made, 1)
                n += 1


def pair_rows():
    import numpy as np

    a = np.full((T0, SPT, F), -1)
    b = np.full((T0, SPT, F), -1)
    for t in range(T0):
        for j in range(SPT):
            s = t * SPT + j
            if s < SHIFTS:
                for f in range(F):
                    g = (f + s) % F
                    a[t, j, f] = f * F + g
                    if s:
                        b[t, j, f] = g * F + f
    return a, b


def kernel(**inputs):
    import numpy as np
    import concourse.bacc as bacc
    from concourse.bass_utils import run_bass_kernel_spmd

    nc = bacc.Bacc("TRN2", target_bir_lowering=False, num_devices=1)
    arrays = {}

    def give(name, a):
        a = np.ascontiguousarray(a)
        arrays[name] = a
        return nc.dram_tensor(name, a.shape, mybir.dt.from_np(a.dtype), kind="ExternalInput").ap()

    w0 = np.asarray(inputs["L0_rec_W0"])
    w0 = np.concatenate([w0, np.zeros((1, L), w0.dtype)])
    pairs = [w0[rows].transpose(1, 2, 0, 3).reshape(P0, T0, L) for rows in pair_rows()]
    args = [
        give("ids", np.asarray(inputs["ids"])),
        [give(f"tbl_{f}", np.asarray(inputs[f"tbl_{f}"])) for f in range(F)],
        give("dense_t", np.asarray(inputs["dense_ctx"]).T),
        give("w_top1", np.asarray(inputs["W_top1"])),
        give("b_top1", np.asarray(inputs["b_top1"]).reshape(M1 // P, P).T),
        give("w_top2", np.asarray(inputs["W_top2"])),
        give("b_top2", np.asarray(inputs["b_top2"]).reshape(M2 // P, P).T),
        give("w_top3", np.asarray(inputs["W_top3"]).reshape(M2 // P, P).T),
        give("w0a", pairs[0]),
        give("w0b", pairs[1]),
        give("w1", np.asarray(inputs["L0_rec_W1"])),
        give("w2", np.asarray(inputs["L0_rec_W2"])),
        give("b0", np.asarray(inputs["L0_rec_b0"])),
        give("b1", np.asarray(inputs["L0_rec_b1"])),
        give("b2", np.asarray(inputs["L0_rec_b2"])),
    ]
    out = nc.dram_tensor("y", (B, 1), F32, kind="ExternalOutput").ap()
    cin_tower(nc, *args, out)
    r = run_bass_kernel_spmd(nc, [arrays], core_ids=[0])
    return r.results[0]["y"]
```

```python
from contextlib import ExitStack

import concourse.bass as bass
from concourse import mybir

F32 = mybir.dt.float32
F32R = mybir.dt.float32r
I32 = mybir.dt.int32
U32 = mybir.dt.uint32
ALU = mybir.AluOpType
ACT = mybir.ActivationFunctionType

P = 128
B, F, D = 1024, 39, 16
L, H = 128, 64
DENSE = 16
COLS = B * D
CH = 512
QS = 4
BC = CH // D
TB = 32
FL = P // TB
MO = TB // D
MI = -(-F // (FL * MO))
GATHERS = MI * MO
CHUNKS = COLS // CH
BLOCKS = CHUNKS // QS
SHIFTS = (F + 1) // 2
SPT = P // F
P0 = SPT * F
T0 = -(-SHIFTS // SPT)
T1 = -(-F // 2)
XROWS = F + SPT * T0
LT = 4
LOADS = T1 // LT
M1, M2 = 512, 256

NAT, SPLIT = range(2)
LAG = 1
EARLY = 1
RING = (4, 4)


class Job:

    def __init__(self, layer, t0, n, kind):
        self.layer, self.t0, self.n, self.kind = layer, t0, n, kind
        self.split = kind != NAT
        self.parts = P0 if layer == 0 else P


GROUPS = {0: "N2 S2 N2 N1",
          1: "N2 S2 N2 N2 S2 N2 N2 S2 N2 N2",
          2: "N2 S2 N2 N2 S2 N2 S2 N2 S2 N2"}
SLOT = [max(int(g[1]) for v in GROUPS.values() for g in v.split() if g[0] == k) for k in "NS"]


def layer_jobs(layer):
    jobs, t = [], 0
    for g in GROUPS[layer].split():
        jobs.append(Job(layer, t, int(g[1]), "NS".index(g[0])))
        t += jobs[-1].n
    assert t == (T0 if layer == 0 else T1)
    return jobs


def plan():
    first, chunk = layer_jobs(0), layer_jobs(1) + layer_jobs(0) + layer_jobs(2)
    per = []
    for kind in (NAT, SPLIT):
        n = 0
        for j in first:
            if j.kind == kind:
                j.n_before = n
                n += 1
        start = n
        for j in chunk:
            if j.kind == kind:
                j.n_before = n
                n += 1
        per.append(n - start)
        assert per[kind] * QS % RING[kind] == 0
    return first, chunk, per


def cin_tower(nc, ids, bases, table, dense_t, w_top1, b_top1, w_top2, b_top2, w_top3,
              w0a, w0b, w1, w2, b0, b1, b2, out):
    first_jobs, chunk_jobs, PER = plan()
    n1, n0 = len(layer_jobs(1)), len(layer_jobs(0))
    jobs1, jobs0, jobs2 = chunk_jobs[:n1], chunk_jobs[n1:n1 + n0], chunk_jobs[n1 + n0:]
    x_dram = nc.dram_tensor("x_rows", (XROWS, COLS), F32, kind="Internal").ap()

    with ExitStack() as ctx:
        def sb(name, shape, dt=F32):
            return ctx.enter_context(nc.sbuf_tensor(name, shape, dt))

        def pb(name):
            return ctx.enter_context(nc.psum_tensor(name, [P, CH], F32))

        def sem(name):
            return ctx.enter_context(nc.semaphore(name))

        ids_all = sb("ids_all", [P, CHUNKS, GATHERS], I32)
        bases_sb = sb("bases_sb", [P, GATHERS], I32)
        rows_all = sb("rows_all", [P, CHUNKS, GATHERS], I32)
        rows_now = sb("rows_now", [P, GATHERS], I32)
        emb = sb("emb", [P, GATHERS * D])
        x_t = sb("x_t", [P, MI * TB])
        x_self = sb("x_self", [P, CH])
        x_shift = sb("x_shift", [P, T0, CH])
        x_pair = sb("x_pair", [P, T1, CH])
        kinds = (NAT, SPLIT)
        z = [[sb(f"z{k}_{i}", [P, SLOT[k], CH]) for i in range(RING[k])] for k in kinds]
        z_hi = [sb(f"z_hi{i}", [P, SLOT[SPLIT], CH], F32R) for i in range(RING[SPLIT])]
        z_lo = [sb(f"z_lo{i}", [P, SLOT[SPLIT], CH], F32R) for i in range(RING[SPLIT])]
        r01 = sb("r01", [P, CH])
        r2 = sb("r2", [P, CH])
        fold = sb("fold", [P, CH])
        sum01 = sb("sum01", [P, B])
        sum2 = sb("sum2", [P, B])
        dense = sb("dense", [DENSE, B])
        bias = [sb(f"bias{i}", [P, 1]) for i in range(3)]
        all_jobs = layer_jobs(0) + layer_jobs(1) + layer_jobs(2)
        w_at, s_at, n_nat, n_split = {}, {}, 0, 0
        for j in all_jobs:
            if j.split:
                s_at[j.layer, j.t0] = n_split
                n_split += j.n
            else:
                w_at[j.layer, j.t0] = n_nat
                n_nat += j.n
        w_nat = sb("w_nat", [P, n_nat, L])
        w_hi = sb("w_hi", [P, n_split, L], F32R)
        w_lo = sb("w_lo", [P, n_split, L], F32R)
        stage = x_pair[:].rearrange("p t (a l) -> p (t a) l", l=L)
        w0_a, w0_b = stage[0:P0, 0:T0, :], stage[0:P0, T0:2 * T0, :]
        w_raw = stage[:, 2 * T0:2 * T0 + n_split, :]

        def w_dst(j):
            return w_raw[:, s_at[j.layer, j.t0]:][:, 0:j.n, :] if j.split else w_nat[:, w_at[j.layer, j.t0]:][:, 0:j.n, :]

        wt1 = x_shift[:, 0:3, :]
        wt2 = x_shift[:, 3:5, :].rearrange("p a (k n) -> p (a k) n", n=M2)
        y_sb = x_shift[0:1, 5:7, :].rearrange("p a n -> p (a n)")
        wt3 = x_self[:, 0:M2 // P]
        bt1 = x_self[:, 8:8 + M1 // P]
        bt2 = x_self[:, 16:16 + M2 // P]
        hid1 = [x_pair[:, 0:4, :], x_pair[:, 4:8, :]]
        hid2 = z[SPLIT]

        h1, h2 = sb("h1", [P, CH]), sb("h2", [P, CH])
        ps = [pb("ps_layer0"), pb("ps_layer1"), pb("ps_layer2")]
        ps_m = [pb(f"ps_m{i}") for i in range(4)]

        ids_in = sem("ids_in")
        small_in = sem("small_in")
        w0_in = sem("w0_in")
        w_in = sem("w_in")
        w0_made = sem("w0_made")
        pads_zero = sem("pads_zero")
        w_hi_made = sem("w_hi_made")
        w_split_made = sem("w_split_made")
        rows_made = sem("rows_made")
        rows_copied = sem("rows_copied")
        emb_in = sem("emb_in")
        t_made = sem("t_made")
        x_stored = sem("x_stored")
        x_self_in = sem("x_self_in")
        x_pair_in = [sem(f"x_pair_in{g}") for g in range(LOADS)]
        z_made = [sem(f"z_made{k}") for k in kinds]
        hi_made = sem("hi_made")
        lo_made = sem("lo_made")
        z_used = [sem(f"z_used{k}") for k in kinds]
        h_made = [sem("h1_made"), sem("h2_made")]
        ps0_free = sem("ps0_free")
        r01_made = sem("r01_made")
        r01_used = sem("r01_used")
        r2_made = sem("r2_made")
        r2_used = sem("r2_used")
        folded = sem("folded")
        top_in = sem("top_in")
        ps_m_made = sem("ps_m_made")
        ps_m_read = sem("ps_m_read")
        out_stored = sem("out_stored")
        ps_free = [ps0_free, r01_made, r2_made]
        passed = {nc.sync: sem("sp_passed"), nc.gpsimd: sem("pool_passed"), nc.tensor: sem("pe_passed")}

        TOP = M1 // P + M2 // P + 1
        W_DMAS = n1 + len(jobs2) + 2
        X_STORE = 16 * (-(-F // MI) - (-(XROWS - F) // MI))

        def place(job, c):
            absent = job.layer == 2 and type(c) is int and c == CHUNKS - 1
            return job.n_before - absent * sum(j.kind == job.kind for j in jobs0)

        def count(job, c):
            return place(job, c) + 1 if c is None else c * PER[job.kind] + place(job, c) + 1

        def ring(job, c, q):
            return (place(job, c) + (0 if c is None else q * PER[job.kind])) % RING[job.kind]

        def wait_made(eng, job, c):
            wait_apart(eng, z_made[job.kind], count(job, c))

        def wait_used(eng, job, c):
            eng.wait_ge(z_used[job.kind], count(job, c) + RING[job.kind])

        def wait_apart(eng, s, value):
            eng.wait_ge(s, value)
            eng.sem_inc(passed[eng], 1)

        def blocks(eng, body):
            with eng.Fori(0, BLOCKS - 1) as i:
                body(i, False)
            body(BLOCKS - 1, True)

        def x_cols(row0, dims, c):
            return bass.AP(x_dram.tensor, c * CH + row0 * COLS,
                           [[s * COLS, n] for s, n in dims] + [[1, CH]])

        block = ctx.enter_context(nc.Block())

        @block.sync
        def _(sp):
            sp.dma_start(ids_all[:], ids).then_inc(ids_in, 16)
            sp.dma_start(bases_sb[:], bases).then_inc(ids_in, 16)
            sp.dma_start(w0_a, w0a).then_inc(w0_in, 16)
            sp.dma_start(w0_b, w0b).then_inc(w0_in, 16)
            for w, jobs in ((w1, layer_jobs(1)), (w2, layer_jobs(2))):
                for j in jobs:
                    full = min(j.n, F // 2 - j.t0)
                    sp.dma_start(w_dst(j)[:, 0:full, :], w[j.t0 * P:(j.t0 + full) * P, :].rearrange(
                        "(t p) l -> p t l", p=P)).then_inc(w_in, 16)
                sp.dma_start(w_dst(j)[0:H, full, :], w[(T1 - 1) * P:F * H, :]).then_inc(w_in, 16)
            for i, b in enumerate((b0, b1, b2)):
                sp.dma_start(bias[i][:], b.rearrange("(p o) -> p o", o=1)).then_inc(small_in, 16)
            sp.dma_start(dense[:], dense_t).then_inc(small_in, 16)

            def store_x(c):
                wait_apart(sp, t_made, c + 1)
                for first, end in ((0, F), (F, XROWS)):
                    for u in range(FL * MO):
                        n = min(MI, end - first - u * MI)
                        if n > 0:
                            dst = bass.AP(x_dram.tensor, c * CH + (first + u * MI) * COLS,
                                          [[BC, D], [COLS, n], [1, BC]])
                            sp.dma_start(dst, x_t[u * D:(u + 1) * D, 0:n * BC].rearrange(
                                "d (f b) -> d f b", b=BC)).then_inc(x_stored, 16)

            def load_shift(c):
                for j in range(SPT):
                    rows = slice(j * F, (j + 1) * F)
                    sp.dma_start(x_self[rows], x_cols(0, [[1, F]], c)).then_inc(x_self_in, 16)
                    sp.dma_start(x_shift[rows], x_cols(j, [[1, F], [SPT, T0]], c)).then_inc(x_self_in, 16)

            def load_pair(g, c):
                t = g * LT
                for odd in range(2):
                    sp.dma_start(x_pair[odd * H:(odd + 1) * H, t:t + LT, :],
                                 x_cols(2 * t + odd, [[0, H], [2, LT]], c)).then_inc(x_pair_in[g], 16)

            def load_top():
                for k in range(2):
                    sp.dma_start(wt1[:, k, :], w_top1[k * P:(k + 1) * P, :]).then_inc(top_in, 16)
                sp.dma_start(wt1[0:DENSE, 2, :], w_top1[2 * P:, :]).then_inc(top_in, 16)
                sp.dma_start(wt2, w_top2.rearrange("(k p) n -> p k n", p=P)).then_inc(top_in, 16)
                sp.dma_start(wt3, w_top3).then_inc(top_in, 16)
                sp.dma_start(bt1, b_top1).then_inc(top_in, 16)
                sp.dma_start(bt2, b_top2).then_inc(top_in, 16)

            store_x(0)
            sp.wait_ge(x_stored, X_STORE)
            load_shift(0)
            sp.wait_ge(w_split_made, 1)
            for g in range(LOADS):
                load_pair(g, 0)
            store_x(1)
            for j in first_jobs:
                wait_made(sp, j, None)

            def body(i, last):
                for q in range(QS):
                    c = i * QS + q
                    if last and q == QS - 1:
                        load_top()
                        break
                    wait_apart(sp, x_stored, X_STORE * (c + 2))
                    load_shift(c + 1)
                    loaded = 0
                    for n, j in enumerate(jobs2):
                        wait_made(sp, j, c)
                        if n == 0:
                            for j0 in jobs0:
                                wait_made(sp, j0, c)
                            if not (last and q == QS - 2):
                                store_x(c + 2)
                        while loaded < LOADS and (loaded + 1) * LT <= j.t0 + j.n:
                            load_pair(loaded, c + 1)
                            loaded += 1

            blocks(sp, body)

            sp.wait_ge(ps_m_read, 2 * TOP)
            sp.dma_start(out.rearrange("b o -> o b"), y_sb).then_inc(out_stored, 16)
            sp.wait_ge(out_stored, 16)

        @block.gpsimd
        def _(pool):
            pool.sem_inc(r01_used, 1)
            pool.sem_inc(r2_used, 1)
            pool.wait_ge(ids_in, 32)
            nc.gpsimd.tensor_tensor(rows_all[:], ids_all[:],
                                    bases_sb[:].rearrange("p (o m) -> p o m", o=1).broadcast_to([P, CHUNKS, GATHERS]),
                                    ALU.add).then_inc(rows_made, 1)
            pool.wait_ge(rows_made, 1)

            def gather(c):
                if not (type(c) is int and c == 0):
                    wait_apart(pool, t_made, c)
                nc.gpsimd.tensor_copy(rows_now[:], rows_all[:, bass.ds(c, 1), :].rearrange(
                    "p o m -> p (o m)")).then_inc(rows_copied, 1)
                wait_apart(pool, rows_copied, c + 1)
                for m in range(GATHERS):
                    nc.gpsimd.indirect_dma_start(
                        out=emb[:, m * D:(m + 1) * D], out_offset=None, in_=table,
                        in_offset=bass.IndirectOffsetOnAxis(ap=rows_now[:, m:m + 1].bitcast(U32), axis=0),
                    ).then_inc(emb_in, 16)

            for c in range(3):
                gather(c)

            def sum_dims(which, total, r, made, used, c):
                wait_apart(pool, made, c + 2)
                n, level = CH // 2, 0
                nc.gpsimd.tensor_tensor(fold[:, 0:n], r[:, 0:n], r[:, n:2 * n], ALU.add).then_inc(used, 1)
                wait_apart(pool, used, c + 2)
                at = 0
                while n > 2 * BC:
                    n //= 2
                    nc.gpsimd.tensor_tensor(fold[:, at + 2 * n:at + 3 * n], fold[:, at:at + n],
                                            fold[:, at + n:at + 2 * n], ALU.add).then_inc(folded, 1)
                    at, level = at + 2 * n, level + 1
                    wait_apart(pool, folded, c * 6 + which * 3 + level)
                nc.gpsimd.tensor_tensor(total[:, bass.ds(c * BC, BC)], fold[:, at:at + BC],
                                        fold[:, at + BC:at + 2 * BC], ALU.add).then_inc(folded, 1)
                wait_apart(pool, folded, c * 6 + which * 3 + 3)

            def body(i, last):
                for q in range(QS):
                    c = i * QS + q
                    sum_dims(0, sum01, r01, r01_made, r01_used, c)
                    if not (last and q + 3 >= QS):
                        gather(c + 3)
                    sum_dims(1, sum2, r2, r2_made, r2_used, c)

            blocks(pool, body)

        @block.scalar
        def _(act):
            for free in ps_free:
                act.sem_inc(free, 1)
            act.wait_ge(w0_made, 2)
            act.wait_ge(w_in, W_DMAS * 16)
            nc.scalar.activation(w_hi[:], w_raw, ACT.Copy).then_inc(w_hi_made, 1)
            act.wait_ge(small_in, 64)

            def split_hi(job, c, q):
                if job.split:
                    n, kind = count(job, c), job.kind
                    act.wait_ge(z_made[kind], n)
                    act.wait_ge(z_used[kind], n)
                    k = ring(job, c, q)
                    nc.scalar.activation(z_hi[k][0:job.parts, 0:job.n, :], z[kind][k][0:job.parts, 0:job.n, :],
                                         ACT.Copy).then_inc(hi_made, 1)

            def relu_h(layer, h, last_job, c):
                wait_used(act, last_job, c)
                nc.scalar.activation(h[0:H, :], ps[layer][0:H, :], ACT.Relu, bias=bias[layer][0:H, :])
                nc.scalar.activation(h[H:P, :], ps[layer][0:H, :], ACT.Relu,
                                     bias=bias[layer][0:H, :]).then_inc(h_made[layer], 1)

            def relu_direct0(c):
                act.wait_ge(r01_used, c + 1)
                nc.scalar.activation(r01[0:H, :], ps[0][H:P, :], ACT.Relu,
                                     bias=bias[0][H:P, :]).then_inc(ps_free[0], 1)

            def relu2(c):
                wait_used(act, jobs2[-1], c)
                act.wait_ge(r2_used, c + 1)
                nc.scalar.activation(r2[:], ps[2][:], ACT.Relu, bias=bias[2][:]).then_inc(r2_made, 1)

            last_split = [j for j in jobs2 if j.split][-1]
            assert last_split.t0 >= M1 // P

            def relu_top(n, to, bias_m, m):
                act.wait_ge(ps_m_made, n + 1)
                nc.scalar.activation(to, ps_m[n % 4][:], ACT.Relu, bias=bias_m[:, m:m + 1]).then_inc(ps_m_read, 1)

            early = [j for j in jobs1 if j.split][:EARLY]
            for j in first_jobs:
                split_hi(j, None, 0)
            relu_h(0, h1, first_jobs[-1], None)
            for j in early:
                split_hi(j, 0, 0)

            def body(i, last):
                for q in range(QS):
                    c = i * QS + q
                    end = last and q == QS - 1
                    relu_direct0(c)
                    for j in jobs1:
                        if j not in early:
                            split_hi(j, c, q)
                    if not end:
                        for j in jobs0:
                            split_hi(j, c, q)
                    relu_h(1, h2, jobs1[-1], c)
                    nc.scalar.activation(r01[H:P, :], ps[1][H:P, :], ACT.Relu,
                                         bias=bias[1][H:P, :]).then_inc(r01_made, 1)
                    for g, j in enumerate(jobs2):
                        split_hi(j, c, q)
                        if j is last_split and end:
                            act.wait_ge(top_in, 7 * 16)
                            for m in range(M1 // P):
                                relu_top(m, hid1[0][:, m, :], bt1, m)
                        if g == len(jobs2) // 2 and not end:
                            relu_h(0, h1, jobs0[-1], c)
                    if not end:
                        for j in early:
                            split_hi(j, c + 1, q + 1)
                    relu2(c)

            blocks(act, body)

            for half_b in range(2):
                n = half_b * TOP
                if half_b:
                    for m in range(M1 // P):
                        relu_top(n + m, hid1[1][:, m, :], bt1, m)
                for m in range(M2 // P):
                    relu_top(n + M1 // P + m, hid2[half_b][:, m, :], bt2, m)
                act.wait_ge(ps_m_made, n + TOP)
                nc.scalar.activation(y_sb[:, half_b * CH:(half_b + 1) * CH], ps_m[(n + TOP - 1) % 4][0:1, :],
                                     ACT.Copy).then_inc(ps_m_read, 1)

        @block.vector
        def _(dve):
            dve.sem_inc(lo_made, RING[SPLIT])
            nc.vector.memset(w_dst(jobs1[-1])[H:P, jobs1[-1].n - 1, :], 0.0)
            pads = nc.vector.memset(w_dst(jobs2[-1])[H:P, jobs2[-1].n - 1, :], 0.0)
            for j in first_jobs:
                if j.split:
                    pads = nc.vector.memset(w_dst(j)[96:P], 0.0)
            pads.then_inc(pads_zero, 1)
            dve.wait_ge(pads_zero, 1)
            dve.wait_ge(w0_in, 32)
            for j in first_jobs:
                w0_sum = nc.vector.tensor_tensor(w_dst(j)[0:P0], w0_a[:, j.t0:j.t0 + j.n, :],
                                                 w0_b[:, j.t0:j.t0 + j.n, :], ALU.add)
            w0_sum.then_inc(w0_made, 2)

            def split_w_lo():
                dve.wait_ge(w_hi_made, 1)
                nc.vector.tensor_tensor(w_lo[:], w_raw, w_hi[:].bitcast(F32),
                                        ALU.subtract).then_inc(w_split_made, 1)

            def product(job, c, q, x, h):
                n, k = count(job, c), ring(job, c, q)
                if job.split:
                    dve.wait_ge(lo_made, n)
                else:
                    dve.wait_ge(z_used[NAT], n)
                rows = job.parts
                nc.vector.tensor_tensor(z[job.kind][k][0:rows, 0:job.n, :], x,
                                        h.rearrange("p (o n) -> p o n", o=1).broadcast_to([rows, job.n, CH]),
                                        ALU.mult).then_inc(z_made[job.kind], 1)

            def split_lo(job, c, q):
                dve.wait_ge(hi_made, count(job, c))
                k, rows = ring(job, c, q), job.parts
                nc.vector.tensor_tensor(z_lo[k][0:rows, 0:job.n, :], z[SPLIT][k][0:rows, 0:job.n, :],
                                        z_hi[k][0:rows, 0:job.n, :].bitcast(F32),
                                        ALU.subtract).then_inc(lo_made, 1)

            def layer(jobs, c, q, h, wait_x):
                pending = []
                for g, j in enumerate(jobs):
                    wait_x(g)
                    x = x_shift[0:P0, j.t0:j.t0 + j.n, :] if j.layer == 0 else x_pair[:, j.t0:j.t0 + j.n, :]
                    product(j, c, q, x, h)
                    if j.kind == SPLIT:
                        pending.append((g, j))
                    if pending and pending[0][0] <= g - LAG:
                        split_lo(pending.pop(0)[1], c, q)
                for _, j in pending:
                    split_lo(j, c, q)

            def layer0(jobs, c, q, chunk):
                def wait_x(g):
                    if g == 0:
                        dve.wait_ge(x_self_in, 2 * SPT * 16 * (chunk + 1))
                layer(jobs, c, q, x_self[0:P0], wait_x)

            def transpose_x(c):
                dve.wait_ge(emb_in, 16 * GATHERS * (c + 1))
                if not (type(c) is int and c == 0):
                    dve.wait_ge(x_stored, X_STORE * c)
                nc.vector.transpose(x_t[:], emb[:]).then_inc(t_made, 1)

            transpose_x(0)
            split_w_lo()
            transpose_x(1)
            layer0(first_jobs, None, 0, 0)

            def body(i, last):
                for q in range(QS):
                    c = i * QS + q
                    dve.wait_ge(h_made[0], c + 1)

                    def wait_pair(g):
                        j = jobs1[g]
                        for load in range(-(-j.t0 // LT), -(-(j.t0 + j.n) // LT)):
                            dve.wait_ge(x_pair_in[load], 32 * (c + 1))

                    layer(jobs1, c, q, h1[:], wait_pair)
                    if not (last and q == QS - 1):
                        layer0(jobs0, c, q, c + 1)
                    if not (last and q >= QS - 2):
                        transpose_x(c + 2)
                    dve.wait_ge(h_made[1], c + 1)
                    layer(jobs2, c, q, h2[:], lambda g: None)

            blocks(dve, body)

        @block.tensor
        def _(pe):
            for k in kinds:
                pe.sem_inc(z_used[k], RING[k])

            def contract(jobs, c, q, bank, free):
                pe.wait_ge(ps_free[bank], free)
                for j in jobs:
                    n, k, rows = count(j, c), ring(j, c, q), j.parts
                    if j.split:
                        pe.wait_ge(lo_made, n + RING[j.kind])
                        s = s_at[j.layer, j.t0]
                        passes = ((w_hi, s, z_hi[k]), (w_lo, s, z_hi[k]), (w_hi, s, z_lo[k]))
                    else:
                        pe.wait_ge(z_made[NAT], n)
                        passes = ((w_nat, w_at[j.layer, j.t0], z[NAT][k]),)
                    for t in range(j.n):
                        for p, (w, at, v) in enumerate(passes):
                            mm = nc.tensor.matmul(
                                ps[bank][:], w[0:rows, at + t, :], v[0:rows, t, :],
                                start=j is jobs[0] and t == 0 and p == 0,
                                stop=j is jobs[-1] and t == j.n - 1 and p == len(passes) - 1)
                    mm.then_inc(z_used[j.kind], 1)

            pe.wait_ge(w0_made, 2)
            pe.wait_ge(w_split_made, 1)
            contract(first_jobs, None, 0, 0, 1)
            pe.wait_ge(w_in, W_DMAS * 16)

            def top(n, terms, first=True, last=True):
                if first and n >= 4:
                    pe.wait_ge(ps_m_read, n - 3)
                for k, (w, v) in enumerate(terms):
                    mm = nc.tensor.matmul(ps_m[n % 4][0:w.shape[-1], :], w, v, start=first and k == 0,
                                          stop=last and k == len(terms) - 1)
                if last:
                    mm.then_inc(ps_m_made, 1)

            def maps01(half_b, m):
                cols = slice(half_b * CH, (half_b + 1) * CH)
                return [(wt1[0:DENSE, 2, m * P:(m + 1) * P], dense[:, cols]), (wt1[:, 0, m * P:(m + 1) * P], sum01[:, cols])]

            def maps2(half_b, m):
                return [(wt1[:, 1, m * P:(m + 1) * P], sum2[:, half_b * CH:(half_b + 1) * CH])]

            def hidden2_y(half_b):
                n = half_b * TOP + M1 // P
                pe.wait_ge(ps_m_read, n)
                for m in range(M2 // P):
                    top(n + m, [(wt2[:, k, m * P:(m + 1) * P], hid1[half_b][:, k, :]) for k in range(M1 // P)])
                n += M2 // P
                pe.wait_ge(ps_m_read, n)
                top(n, [(wt3[:, k:k + 1], hid2[half_b][:, k, :]) for k in range(M2 // P)])

            def body(i, last):
                for q in range(QS):
                    c = i * QS + q
                    contract(jobs1, c, q, 1, c + 1)
                    if not (last and q == QS - 1):
                        contract(jobs0, c, q, 0, c + 2)
                    else:
                        pe.wait_ge(top_in, 7 * 16)
                        pe.wait_ge(folded, 6 * CHUNKS // 2)
                        for m in range(M1 // P):
                            top(m, maps01(0, m) + maps2(0, m))
                    contract(jobs2, c, q, 2, c + 1)

            blocks(pe, body)

            hidden2_y(0)
            pe.wait_ge(folded, 6 * CHUNKS - 3)
            for m in range(M1 // P):
                top(TOP + m, maps01(1, m), last=False)
            pe.wait_ge(folded, 6 * CHUNKS)
            for m in range(M1 // P):
                top(TOP + m, maps2(1, m), first=False)
            hidden2_y(1)


def pair_rows():
    import numpy as np

    a = np.full((T0, SPT, F), -1)
    b = np.full((T0, SPT, F), -1)
    for t in range(T0):
        for j in range(SPT):
            s = t * SPT + j
            if s < SHIFTS:
                for f in range(F):
                    g = (f + s) % F
                    a[t, j, f] = f * F + g
                    if s:
                        b[t, j, f] = g * F + f
    return a, b


def kernel(**inputs):
    import numpy as np
    import concourse.bacc as bacc
    from concourse.bass_utils import run_bass_kernel_spmd

    nc = bacc.Bacc("TRN2", target_bir_lowering=False, num_devices=1)
    arrays = {}

    def give(name, a):
        a = np.ascontiguousarray(a)
        arrays[name] = a
        return nc.dram_tensor(name, a.shape, mybir.dt.from_np(a.dtype), kind="ExternalInput").ap()

    w0 = np.asarray(inputs["L0_rec_W0"])
    w0 = np.concatenate([w0, np.zeros((1, L), w0.dtype)])
    pairs = [w0[rows].transpose(1, 2, 0, 3).reshape(P0, T0, L) for rows in pair_rows()]
    tables = [np.asarray(inputs[f"tbl_{f}"]) for f in range(F)]
    ids = np.asarray(inputs["ids"])
    spare = FL * MO * MI - F
    ids = np.concatenate([ids, np.zeros((B, spare), ids.dtype)], axis=1)
    ids = ids.reshape(CHUNKS, BC, FL, MO, MI).transpose(2, 1, 0, 4, 3).reshape(P, CHUNKS, GATHERS)
    first = np.array([sum(t.shape[0] for t in tables[:f]) for f in range(F)] + [0] * spare, ids.dtype)
    first = np.broadcast_to(first.reshape(FL, 1, MO, MI).transpose(0, 1, 3, 2), (FL, BC, MI, MO)).reshape(P, GATHERS)
    args = [
        give("ids", ids),
        give("bases", first),
        give("table", np.concatenate(tables)),
        give("dense_t", np.asarray(inputs["dense_ctx"]).T),
        give("w_top1", np.asarray(inputs["W_top1"])),
        give("b_top1", np.asarray(inputs["b_top1"]).reshape(M1 // P, P).T),
        give("w_top2", np.asarray(inputs["W_top2"])),
        give("b_top2", np.asarray(inputs["b_top2"]).reshape(M2 // P, P).T),
        give("w_top3", np.asarray(inputs["W_top3"]).reshape(M2 // P, P).T),
        give("w0a", pairs[0]),
        give("w0b", pairs[1]),
        give("w1", np.asarray(inputs["L0_rec_W1"])),
        give("w2", np.asarray(inputs["L0_rec_W2"])),
        give("b0", np.asarray(inputs["L0_rec_b0"])),
        give("b1", np.asarray(inputs["L0_rec_b1"])),
        give("b2", np.asarray(inputs["L0_rec_b2"])),
    ]
    out = nc.dram_tensor("y", (B, 1), F32, kind="ExternalOutput").ap()
    cin_tower(nc, *args, out)
    r = run_bass_kernel_spmd(nc, [arrays], core_ids=[0])
    return r.results[0]["y"]
```
